# Optimizing a Trainium2 kernel written in Bass

```python
import numpy as np
import jax
import jax.numpy as jnp

def _softmax(x, axis=-1):
    return jax.nn.softmax(x, axis=axis)

def _gelu(x):
    return jax.nn.gelu(x, approximate=True)

def _silu(x):
    return jax.nn.silu(x)

def _sigmoid(x):
    return jax.nn.sigmoid(x)

def _layernorm(x, axis=-1, eps=1e-05):
    m = jnp.mean(x, axis=axis, keepdims=True)
    v = jnp.var(x, axis=axis, keepdims=True)
    return (x - m) / jnp.sqrt(v + eps)

def _scatter_add(tgt, idx, src, axis=0):
    return tgt.at[idx].add(src)

def _segment_sum(src, seg, n):
    return jax.ops.segment_sum(src, seg, n)
kernel_name = 'mk_prb_d1_jaxref_r8_899204'

def setup_inputs(seed: int=0):
    np.random.seed(seed)
    _w = jnp.asarray

    def _L0_attn_setup():
        import jax, jax.numpy as jnp
        import numpy as np
        import math
        B, T, D, H = (2, 256, 128, 16)
        DH = D // H

        def _rope_tensor(t, dh):
            pos = jnp.arange(t, dtype=jnp.float32)
            angles = pos[:, None] / 10000.0 ** (jnp.arange(0, dh, 2, dtype=jnp.float32) / dh)
            rope = jnp.stack([jnp.cos(angles), jnp.sin(angles)], axis=-1).reshape(t, dh)
            return rope

        def _rotate(x):
            return jnp.stack([-x[..., 1::2], x[..., 0::2]], axis=-1).reshape(x.shape)
        key = jax.random.key(seed)
        k1, k2, k3 = jax.random.split(key, 3)
        x = jax.random.normal(k1, (B, T, D), dtype=jnp.float32)
        Wqkv = jax.random.normal(k2, (3 * D, D), dtype=jnp.float32) * 0.02
        bqkv = jnp.zeros((3 * D,), dtype=jnp.float32)
        Wproj = jax.random.normal(k3, (D, D), dtype=jnp.float32) * 0.02
        bproj = jnp.zeros((D,), dtype=jnp.float32)
        return {'x': x, 'Wqkv': Wqkv, 'bqkv': bqkv, 'Wproj': Wproj, 'bproj': bproj}
    _L0_attn_in = _L0_attn_setup()

    def _L0_ffn_setup():
        import jax, jax.numpy as jnp
        import numpy as np
        NUM_EXPERTS = 8
        NUM_SELECTED = 2
        EXPERT_CAPACITY = 64
        NUM_GROUPS = 8

        def _routing(xg, w_router):
            G, T, H = xg.shape
            logits = jnp.einsum('gth,he->gte', xg, w_router)
            probs = jax.nn.softmax(logits, axis=-1)
            _gate, idx = jax.lax.top_k(probs, NUM_SELECTED)
            idx_kt = jnp.swapaxes(idx, 1, 2).reshape(G, -1)
            expert_mask = jax.nn.one_hot(idx_kt, NUM_EXPERTS, dtype=jnp.int32)
            priority = jnp.cumsum(expert_mask, axis=1) * expert_mask - 1
            priority = priority.reshape(G, NUM_SELECTED, T, NUM_EXPERTS)
            priority = jnp.swapaxes(priority, 1, 2).max(axis=2)
            dispatch = jax.nn.one_hot(priority, EXPERT_CAPACITY, dtype=xg.dtype)
            combine = probs[..., None] * dispatch
            return (dispatch, combine)
        key = jax.random.key(seed)
        k1, k2, k3, k4 = jax.random.split(key, 4)
        B, S, H, F = (8, 256, 128, 512)
        return {'x': jax.random.normal(k1, (B, S, H), jnp.float32), 'w_router': jax.random.normal(k2, (H, NUM_EXPERTS), jnp.float32) * 0.02, 'wi': jax.random.normal(k3, (NUM_EXPERTS, H, F), jnp.float32) * 0.02, 'wo': jax.random.normal(k4, (NUM_EXPERTS, F, H), jnp.float32) * 0.02}
    _L0_ffn_in = _L0_ffn_setup()
    _d = {'L0_attn_x': _L0_attn_in['x'], 'L0_attn_Wqkv': _L0_attn_in['Wqkv'], 'L0_attn_bqkv': _L0_attn_in['bqkv'], 'L0_attn_Wproj': _L0_attn_in['Wproj'], 'L0_attn_bproj': _L0_attn_in['bproj'], 'L0_ffn_w_router': _L0_ffn_in['w_router'], 'L0_ffn_wi': _L0_ffn_in['wi'], 'L0_ffn_wo': _L0_ffn_in['wo']}
    _x0 = _d['L0_attn_x']
    _d['L0_attn_x'] = jax.random.normal(jax.random.fold_in(jax.random.key(seed), 1), (32, 256, 128), dtype=_x0.dtype)
    del _x0
    return _d

def reference(L0_attn_x, L0_attn_Wqkv, L0_attn_bqkv, L0_attn_Wproj, L0_attn_bproj, L0_ffn_w_router, L0_ffn_wi, L0_ffn_wo):

    def _L0_attn_ref(x, Wqkv, bqkv, Wproj, bproj):
        import jax, jax.numpy as jnp
        import numpy as np
        import math
        B, T, D, H = (2, 256, 128, 16)
        DH = D // H

        def _rope_tensor(t, dh):
            pos = jnp.arange(t, dtype=jnp.float32)
            angles = pos[:, None] / 10000.0 ** (jnp.arange(0, dh, 2, dtype=jnp.float32) / dh)
            rope = jnp.stack([jnp.cos(angles), jnp.sin(angles)], axis=-1).reshape(t, dh)
            return rope

        def _rotate(x):
            return jnp.stack([-x[..., 1::2], x[..., 0::2]], axis=-1).reshape(x.shape)
        b, t, d = x.shape
        qkv = x @ Wqkv.T + bqkv
        qkv = qkv.reshape(b, t, H, 3 * DH).transpose(0, 2, 1, 3)
        q, k, v = jnp.split(qkv, 3, axis=-1)
        rope = _rope_tensor(t, DH)
        q = q * rope + _rotate(q) * (1.0 - rope)
        k = k * rope + _rotate(k) * (1.0 - rope)
        att = jnp.einsum('bhtd,bhsd->bhts', q, k) * (1.0 / math.sqrt(DH))
        causal = jnp.tril(jnp.ones((t, t), dtype=bool))
        att = jnp.where(causal, att, -jnp.inf)
        att = jax.nn.softmax(att, axis=-1)
        y = jnp.einsum('bhts,bhsd->bhtd', att, v)
        y = y.transpose(0, 2, 1, 3).reshape(b, t, d)
        return y @ Wproj.T + bproj

    def _L0_ffn_ref(x, w_router, wi, wo):
        import jax, jax.numpy as jnp
        import numpy as np
        NUM_EXPERTS = 8
        NUM_SELECTED = 2
        EXPERT_CAPACITY = 64
        NUM_GROUPS = 8

        def _routing(xg, w_router):
            G, T, H = xg.shape
            logits = jnp.einsum('gth,he->gte', xg, w_router)
            probs = jax.nn.softmax(logits, axis=-1)
            _gate, idx = jax.lax.top_k(probs, NUM_SELECTED)
            idx_kt = jnp.swapaxes(idx, 1, 2).reshape(G, -1)
            expert_mask = jax.nn.one_hot(idx_kt, NUM_EXPERTS, dtype=jnp.int32)
            priority = jnp.cumsum(expert_mask, axis=1) * expert_mask - 1
            priority = priority.reshape(G, NUM_SELECTED, T, NUM_EXPERTS)
            priority = jnp.swapaxes(priority, 1, 2).max(axis=2)
            dispatch = jax.nn.one_hot(priority, EXPERT_CAPACITY, dtype=xg.dtype)
            combine = probs[..., None] * dispatch
            return (dispatch, combine)
        B, S, H = x.shape
        T = B * S // NUM_GROUPS
        xg = x.reshape(NUM_GROUPS, T, H)
        dispatch, combine = _routing(xg, w_router)
        expert_in = jnp.einsum('gth,gtec->gech', xg, dispatch)
        h = jax.nn.gelu(jnp.einsum('gech,ehf->gecf', expert_in, wi))
        expert_out = jnp.einsum('gecf,efh->gech', h, wo)
        out = jnp.einsum('gech,gtec->gth', expert_out, combine)
        return out.reshape(B, S, H)
    x = L0_attn_x
    xn = _layernorm(x, axis=-1)
    x = x + _L0_attn_ref(xn, L0_attn_Wqkv, L0_attn_bqkv, L0_attn_Wproj, L0_attn_bproj) + _L0_ffn_ref(xn, L0_ffn_w_router, L0_ffn_wi, L0_ffn_wo)
    return x

_drawn_inputs = setup_inputs


def setup_inputs(seed=0):
    import zlib

    import numpy as np

    out = dict(_drawn_inputs(seed))
    spreads = {'L0_attn_bqkv': (0.0, 0.357), 'L0_attn_bproj': (0.0, 0.1)}
    factors = {'L0_attn_Wqkv': 7.0, 'L0_ffn_w_router': 8.0, 'L0_ffn_wi': 8.0, 'L0_ffn_wo': 8.0}
    for name, (base, spread) in spreads.items():
        noise = np.random.default_rng([zlib.crc32(name.encode()), seed]).standard_normal(out[name].shape)
        drawn = base * np.exp(spread * noise) if base else spread * noise
        out[name] = jnp.asarray(drawn.astype(out[name].dtype))
    for name, factor in factors.items():
        out[name] = (out[name] * factor).astype(out[name].dtype)
    return out
```

```python
from contextlib import ExitStack

import numpy as np

import concourse.bass as bass
from concourse import mybir

F32 = mybir.dt.float32
F16 = mybir.dt.float16
I32 = mybir.dt.int32
ALU = mybir.AluOpType
ACT = mybir.ActivationFunctionType
AX = mybir.AxisListType.X

P = 128
B, T, D, H = 32, 256, 128, 16
DH = D // H
NTOK = B * T
TILES = NTOK // P
PAIRS = B // 2
PT = 2 * T
TP = PT // P
G = 4
HG = H // G
TERMS = 3
KR_ROWS = TERMS * HG * DH
M_ROWS = KR_ROWS + HG
CH = 32
NCH = T // CH
NE, CAP, FF = 8, 64, 512
NGRP = 8
SLOTS = NE * NGRP * CAP
ROW = D + 4
XROW = ROW + 2
EPS = 1e-5
SCALE = float(DH) ** -0.5
MSCALE = 256.0
BIG = 32768.0
NOWHERE = 1.0e6


def constants():
    pos = np.arange(T, dtype=np.float32)
    ang = pos[:, None] / (np.float32(10000.0) ** (np.arange(0, DH, 2, dtype=np.float32) / np.float32(DH)))
    rope = np.stack([np.cos(ang), np.sin(ang)], axis=-1).reshape(T, DH).astype(np.float32)
    rt = np.tile(rope.T, (H, 1))
    sign = np.where(np.arange(P) % 2 == 0, -1.0, 1.0).astype(np.float32)[:, None]
    rows = np.arange(P)
    f = {}
    f["rope"] = rt
    f["rope1"] = (np.float32(1.0) - rt) * sign
    f["ident"] = np.eye(P, dtype=np.float32)
    f["order"] = np.tile(8.0 - np.arange(NE), (P, TILES))
    f["grp"] = np.tile(np.arange(TILES) // (TILES // NGRP) * CAP, (P, 1))
    f["tok"] = rows[:, None] + P * np.arange(TILES)[None, :]
    f["slot_e"] = np.tile(np.arange(SLOTS // P) // (SLOTS // P // NE), (P, 1))
    f["head_rows"] = np.stack([(rows < KR_ROWS) & (rows // DH % HG == hh) for hh in range(HG)], 1)
    f["eps"] = np.full((P, 1), EPS)
    at, parts = {}, []
    n = 0
    for name, a in f.items():
        at[name] = (n, n + a.shape[1])
        n += a.shape[1]
        parts.append(a.astype(np.float32))
    packed = np.concatenate(parts, axis=1)

    before = (rows[:, None] < rows[None, :]).astype(np.float16)
    q, r = np.arange(CH), np.arange(CH)
    kmask = np.where(q[None, :] > r[:, None], -BIG, 0.0)
    return {
        "cf": packed,
        "before": before,
        "cmask": np.where(rows[:, None] > rows[None, :], -BIG, 0.0).astype(np.float16),
        "big_id": (np.eye(P) * BIG).astype(np.float16),
        "kmask": np.tile(kmask, (1, G * PT // CH)).astype(np.float16),
        "qhot": np.tile(np.eye(CH) * BIG, (1, G * NCH * HG)).astype(np.float16),
        "kones": np.stack([np.where(np.arange(HG)[:, None] == hh, MSCALE, 0.0) * np.ones((1, G * PT)) for hh in range(HG)]).astype(np.float16),
    }, at


def sweep(eng, body, start, loop_from, loop_to, end):
    for n in range(start, loop_from):
        body(n, n % 2, n // 2)
    with eng.Fori(0, (loop_to - loop_from) // 2) as it:
        for k in range(2):
            n0 = loop_from + k
            body(it * 2 + n0, n0 % 2, it + n0 // 2)
    for n in range(loop_to, end):
        body(n, n % 2, n // 2)


def within(n, lo, hi):
    return lo <= n < hi if isinstance(n, int) else True


def need(eng, sem, value):
    if not isinstance(value, int) or value > 0:
        eng.wait_ge(sem, value)


def hold(eng, sem, value, seen):
    if not isinstance(value, int):
        eng.wait_ge(sem, value)
        eng.sem_inc(seen, 1)
    elif value > 0:
        eng.wait_ge(sem, value)


def pair_of(view, n):
    return view[n] if isinstance(n, int) else view[bass.ds(n, 1)].rearrange("a p t d -> p (a t) d")


def attend_and_mix(nc, a, at):
    ctx = ExitStack()
    with ctx:
        def sb(name, shape, dt=F32):
            return ctx.enter_context(nc.sbuf_tensor(name, shape, dt))

        def sem(name):
            return ctx.enter_context(nc.semaphore(name))

        def sem2(name):
            return [sem(f"{name}{i}") for i in range(2)]

        qk_dram = nc.dram_tensor("qk_parts", (PAIRS, 4, P, PT), F16, kind="Internal").ap()
        m_dram = nc.dram_tensor("maxima", (2, 2, P, CH), F16, kind="Internal").ap()
        slot_dram = nc.dram_tensor("slot_rows", (SLOTS, ROW), F32, kind="Internal").ap()
        moe_dram = nc.dram_tensor("moe_rows", (2 * NTOK, D), F32, kind="Internal").ap()

        cf = sb("cf_sb", [P, a["cf"].shape[1]])
        def const(name):
            return cf[:, at[name][0]:at[name][1]]
        before = sb("before_sb", [P, P], F16)
        ones16 = sb("ones16", [P, P], F16)
        cmask = sb("cmask_sb", [P, P], F16)
        big_id = sb("big_id_sb", [P, P], F16)
        w_qk = sb("w_qk_sb", [P, 4, P])
        w_vr = sb("w_vr_sb", [P, D + NE])
        w_o = sb("w_o_sb", [P, D])
        b_qk = sb("b_qk_sb", [P, 4])
        b_v = sb("b_v_sb", [P, 1])
        bv_wide = sb("bv_wide", [P, P])
        b_o = sb("b_o_sb", [P, D])
        b_all = sb("b_all", [P, D])

        xd = sb("xd", [P, TILES, XROW])
        v_all = sb("v_all", [P, TILES, D])

        x_in = [sb(f"x_in{i}", [P, TP, D]) for i in range(2)]
        xn = [sb(f"xn{i}", [P, TP, D]) for i in range(2)]
        xt = [sb(f"xt{i}", [P, PT]) for i in range(2)]
        stats = sb("stats", [P, TP, 6])
        mv = sb("mv", [P, TP, 2])
        dev = sb("dev", [P, TP])
        rstd = sb("rstd", [P, TP])
        shared = sb("shared", [P, 8 * PT])
        rot = [shared[:, 4 * PT * i:4 * PT * (i + 1)].rearrange("p (j t) -> p j t", j=4) for i in range(2)]
        p0 = [shared[:, HG * T * i:HG * T * (i + 1)].rearrange("p (h t) -> p h t", h=HG) for i in range(2)]
        p1 = [shared[:, 4 * PT + PT * i:4 * PT + PT * (i + 1)].rearrange("p (h t) -> p h t", h=HG) for i in range(2)]
        x_res = [shared[:, 6 * PT + PT * i:6 * PT + PT * (i + 1)].rearrange("p (t d) -> p t d", t=TP) for i in range(2)]
        parts = [sb(f"parts{i}", [P, 4, PT], F16) for i in range(2)]

        qb = [sb(f"qb{i}", [P, G, PT], F16) for i in range(2)]
        kr = [sb(f"kr{i}", [P, G, PT], F16) for i in range(2)]
        qm = [sb(f"qm{i}", [P, G, PT], F16) for i in range(2)]
        kp = [[sb(f"kp{i}{hh}", [P, G, PT], F16) for hh in range(HG)] for i in range(2)]
        qbd = [sb(f"qbd{i}", [P, G, NCH, HG, CH], F16) for i in range(2)]
        mx = sb("mx", [P, 2, G, NCH])
        mx16 = sb("mx16", [P, 2, G * NCH], F16)
        mxt = sb("mxt", [P, 2, CH], F16)
        vp = [sb(f"vp{i}", [P, 2, H, CH]) for i in range(2)]
        y_u = sb("y_u", [P, 2, T])
        y_r = sb("y_r", [P, 2, 2, HG, 3])
        y_n = sb("y_n", [P, 2, D])
        y_t = sb("y_t", [P, T])
        stage = [sb(f"stage{i}", [P, TP, XROW]) for i in range(2)]

        def room(t, k, n=TILES * NE):
            return t[:, k, 0:n]
        lg = sb("lg", [P, TILES, NE])

        PS = ctx.enter_context(nc.psum_tensor("PS", [P, 8 * 512], F32))

        def bank(k, n=1):
            return PS[:, 512 * k:512 * (k + n)]

        s_cf = sem("const_loaded"); s_w = sem("weights_loaded"); s_init = sem("patterns_loaded")
        s_zero = sem("zeroed"); s_vzero = sem("v_zeroed"); s_vones = sem("v_ones"); s_fill = sem("slot_fill_set"); s_moe0 = sem("moe_rows_zeroed"); s_slot0 = sem("slot_rows_set")
        x_loaded = sem2("x_loaded"); xd_copied = sem2("xd_copied"); parts_stored = sem2("parts_stored")
        stats_done = sem("stats_done"); mv_done = sem("mv_done"); dev_done = sem("dev_done")
        rstd_done = sem("rstd_done"); xn_done = sem("xn_done")
        xt_ps = sem("xt_ps"); xt_done = sem("xt_done")
        v_ps = sem("v_ps"); v_kept = sem("v_kept"); lg_kept = sem("lg_kept")
        proj_ps = sem("proj_ps"); rot_done = sem("rot_done"); sum_done = sem("sum_done")
        high_done = sem("high_done"); low_done = sem("low_done")
        bv_done = sem("bv_wide_done"); ball_ps = sem("ball_ps"); ball_done = sem("ball_done")
        r_dve = sem("route_dve"); r_exp = sem("route_exp"); r_hot = sem("route_hot"); r_ps = sem("route_ps")
        routed = sem("routed")
        seen_sp = sem("seen_sp"); seen_dve = sem("seen_dve"); seen_pool = sem("seen_pool")

        qb_loaded = sem2("qb_loaded"); kr_loaded = sem2("kr_loaded"); qm_loaded = sem2("qm_loaded"); kp_loaded = sem2("kp_loaded")
        m_out = sem2("m_out"); m_in = sem2("m_in"); stage_in = sem2("stage_in"); scattered = sem2("scattered")
        xres_in = sem2("xres_in"); xres_done = sem("xres_done")
        qbd_done = sem("qbd_done"); mx_ps = sem("mx_ps"); mx_done = sem("mx_done"); m16_done = sem("m16_done"); mt_done = sem("mt_done")
        s0_ps = sem("s0_ps"); s1_ps = sem("s1_ps"); p0_exp = sem("p0_exp"); p1_exp = sem("p1_exp")
        pv_unit = sem("pv_unit")
        vp_done = [sem("vp_done0"), sem("vp_done1")]
        yu_done = sem("yu_done"); ytr_ps = sem("ytr_ps"); yr_done = sem("yr_done"); yn_done = sem("yn_done")
        yt_ps = sem("yt_ps"); yt_done = sem("yt_done"); out_ps = sem("out_ps"); res_done = sem("res_done")

        sl_in = sem2("sl_in"); we_in = sem2("we_in"); d_meta = sem("d_meta"); idx_done = sem("idx_done")
        st_ps = sem("st_ps"); st_done = sem("st_done"); h_ps = sem("h_ps"); h_done = sem("h_done")
        eo_ps = sem("eo_ps"); eo_done = sem("eo_done"); moe_out = sem2("moe_out")
        acc_in = sem2("acc_in"); fin1 = sem("fin1"); fin2 = sem("fin2"); stored = sem2("stored")

        x_v = a["x"].rearrange("(n t p) d -> n p t d", t=TP, p=P)
        out_v = a["out"].rearrange("(n t p) d -> n p t d", t=TP, p=P)
        moe_v = moe_dram.rearrange("(k n t p) d -> k n p t d", k=2, t=TP, p=P)

        SPE = SLOTS // NE // P
        sl = [stage[i] for i in range(2)]
        wi = [qb[i][:, 0:2, :].bitcast(F32).rearrange("p g t -> p (g t)") for i in range(2)]
        wo = [qb[i][:, 2:4, :].bitcast(F32).rearrange("p g t -> p (g t)") for i in range(2)]
        s_t = [xt[i] for i in range(2)]
        h_t = [rot[i] for i in range(2)]
        eo = [xn[i] for i in range(2)]
        acc = [[p0[i][:, 0:2, :].rearrange("p h t -> p (h t)"), p0[i][:, 2:4, :].rearrange("p h t -> p (h t)")] for i in range(2)]
        fin = [x_in[i] for i in range(2)]
        meta = [sb(f"meta{i}", [P, SPE, 4]) for i in range(2)]
        meta_i = [sb(f"meta_i{i}", [P, SPE], I32) for i in range(2)]

        zero_tile = sb("zero_tile", [P, PT])
        slot_fill = sb("slot_fill", [P, ROW])

        block = ctx.enter_context(nc.Block())

        def task_view(t):
            b_, c = divmod(t, NCH)
            i = NCH - 1 - c // 2 if c % 2 == 0 else NCH // 2 - 1 - c // 2
            if i >= NCH // 2:
                return b_, i, bank(3, 2).rearrange("p (g t) -> p g t", g=G)
            return b_, i, bank(5).rearrange("p (g t) -> p g t", g=G)

        @block.sync
        def _(sp):
            sp.dma_start(cf[:], a["cf"]).then_inc(s_cf, 16)
            sp.dma_start(w_qk[:], a["w_qk"]).then_inc(s_w, 16)
            sp.dma_start(w_vr[:], a["w_vr"]).then_inc(s_w, 16)
            sp.dma_start(b_qk[:], a["b_qk"]).then_inc(s_w, 16)
            sp.dma_start(b_v[:], a["b_v"]).then_inc(s_w, 16)
            sp.dma_start(w_o[:], a["w_o"]).then_inc(s_w, 16)
            sp.dma_start(b_o[:], a["b_o"]).then_inc(s_w, 16)
            sp.dma_start(before[:], a["before"]).then_inc(s_w, 16)
            sp.dma_start(cmask[:], a["cmask"]).then_inc(s_w, 16)
            sp.dma_start(big_id[:], a["big_id"]).then_inc(s_w, 16)

            sp.wait_ge(s_zero, 10)
            sp.wait_ge(s_fill, 2)
            slot_v = slot_dram.rearrange("(n t p) d -> n p t d", n=PAIRS, p=P)

            def norm(n, u, h):
                if within(n, 0, PAIRS):
                    need(sp, xn_done, (n - 1) * TP)
                    sp.dma_start(x_in[u][:], pair_of(x_v, n)).then_inc(x_loaded[u], 16)
                    for k in range(2):
                        sp.dma_start(pair_of(moe_v[k], n), zero_tile[:].rearrange("p (t d) -> p t d", t=TP)).then_inc(s_moe0, 16)
                    fill = slot_fill[:, None, :].to_broadcast([P, SLOTS // P // PAIRS, ROW])
                    sp.dma_start(pair_of(slot_v, n), fill).then_inc(s_slot0, 16)
                if within(n, 1, PAIRS + 1):
                    v = 1 - u
                    sp.wait_ge(xn_done, n * TP)
                    sp.dma_start(xd[:, bass.ds(n * TP - TP, TP), 0:D], xn[v][:]).then_inc(xd_copied[v], 16)
                if within(n, 3, PAIRS + 3):
                    v = 1 - u
                    sp.wait_ge(low_done, 2 * (n - 2))
                    sp.dma_start(qk_dram[bass.ds(n - 3, 1)].rearrange("a x p t -> p (a x) t"),
                                 parts[v][:]).then_inc(parts_stored[v], 16)

            for n in range(3):
                norm(n, n % 2, n // 2)
            with sp.Fori(0, 6) as it:
                norm(it * 2 + 3, 1, it + 1)
                norm(it * 2 + 4, 0, it + 2)
            for n in range(15, PAIRS + 3):
                norm(n, n % 2, n // 2)
            sp.wait_ge(s_zero, 10)
            for i in range(2):
                sp.dma_start(kr[i][KR_ROWS:P, :, :].rearrange("p g t -> p (g t)"), a["kmask"]).then_inc(s_init, 16)
                sp.dma_start(qbd[i][KR_ROWS:P].rearrange("p g i h q -> p (g i h q)"), a["qhot"]).then_inc(s_init, 16)
                for hh in range(HG):
                    sp.dma_start(kp[i][hh][KR_ROWS:M_ROWS].rearrange("p g t -> p (g t)"), a["kones"][hh]).then_inc(s_init, 16)

            def part_rows(pair, part):
                return qk_dram[pair, part].rearrange("(g r) t -> r g t", g=G) if isinstance(pair, int) else \
                    qk_dram[bass.ds(pair, 1), part].rearrange("a (g r) t -> r (a g) t", g=G)

            Q_HI, Q_LO, K_HI, K_LO = range(4)

            def load_max_operands(n, v):
                for term, part in enumerate((Q_HI, Q_HI, Q_LO)):
                    sp.dma_start(qb[v][32 * term:32 * term + 32], part_rows(n, part)).then_inc(qb_loaded[v], 16)
                for term, part in enumerate((K_HI, K_LO, K_HI)):
                    sp.dma_start(kr[v][32 * term:32 * term + 32], part_rows(n, part)).then_inc(kr_loaded[v], 16)

            def load_main_operands(n, v):
                for term, part in enumerate((Q_HI, Q_HI, Q_LO)):
                    sp.dma_start(qm[v][32 * term:32 * term + 32], part_rows(n, part)).then_inc(qm_loaded[v], 16)
                for term, part in enumerate((K_HI, K_LO, K_HI)):
                    for hh in range(HG):
                        r0 = 32 * term + DH * hh
                        src = part_rows(n, part)[DH * hh:DH * hh + DH]
                        sp.dma_start(kp[v][hh][r0:r0 + DH], src).then_inc(kp_loaded[v], 16)

            sp.wait_ge(parts_stored[0], 16 * PAIRS // 2)
            sp.wait_ge(parts_stored[1], 16 * PAIRS // 2)
            sp.wait_ge(s_init, 16 * 12)
            load_max_operands(0, 0)

            def attend(n, u, h):
                w = 1 - u
                if within(n, -1, PAIRS - 1):
                    need(sp, s1_ps, 8 * n)
                    load_main_operands(n + 1, w)
                if within(n, -1, PAIRS - 2):
                    hold(sp, qbd_done, 8 * (n + 1), seen_sp)
                    hold(sp, mx_ps, 16 * (n + 1), seen_sp)
                    load_max_operands(n + 2, u)
                if within(n, 0, PAIRS):
                    if isinstance(n, int) and n == 0:
                        sp.wait_ge(routed, 1)
                    need(sp, scattered[u], 128 * h)
                    sp.dma_start(stage[u][:], xd[:, bass.ds(n * TP, TP), :]).then_inc(stage_in[u], 16)
                    need(sp, res_done, 2 * (n - 1))
                    sp.dma_start(x_res[u], pair_of(x_v, n)).then_inc(xres_in[u], 16)
                if within(n, -1, PAIRS - 1):
                    for b_ in range(2):
                        sp.wait_ge(mt_done, 2 * (n + 1) + b_ + 1)
                        sp.dma_start(m_dram[w, b_], mxt[:, b_, :]).then_inc(m_out[b_], 16)
                        sp.wait_ge(m_out[b_], 16 * (n + 2))
                        sp.dma_start(qm[w][KR_ROWS:M_ROWS, :, b_ * T:(b_ + 1) * T],
                                     m_dram[w, b_].rearrange("(r g i) q -> r g (i q)", r=HG, g=G)).then_inc(m_in[b_], 16)

            sweep(sp, attend, -1, 1, 13, 16)

            def expert(e):
                u = e % 2
                if e == 0:
                    sp.wait_ge(scattered[0], 128 * PAIRS // 2)
                    sp.wait_ge(scattered[1], 128 * PAIRS // 2)
                    sp.wait_ge(res_done, 2 * PAIRS)
                if e >= 2:
                    sp.wait_ge(eo_ps, e - 1)
                    sp.wait_ge(eo_done, e - 1)
                sp.dma_start(sl[u][:, :, 0:ROW], slot_dram[e * SPE * P:(e + 1) * SPE * P, :]
                             .rearrange("(t p) d -> p t d", p=P)).then_inc(sl_in[u], 16)
                sp.dma_start(wi[u], a["wi"][e]).then_inc(we_in[u], 16)
                sp.dma_start(wo[u].rearrange("p (c d) -> p c d", c=FF // P), a["wo"][e].rearrange("(c p) d -> p c d", p=P)).then_inc(we_in[u], 16)

            for e in range(NE):
                expert(e)

            sp.wait_ge(moe_out[0], 64 * NE // 2)
            sp.wait_ge(moe_out[1], 64 * NE // 2)

            def finish(n, u, h):
                if within(n, 0, PAIRS):
                    need(sp, fin2, n - 1)
                    for k in range(2):
                        src = pair_of(moe_v[k], n)
                        sp.dma_start(acc[u][k].rearrange("p (t d) -> p t d", t=TP), src).then_inc(acc_in[u], 16)
                if within(n, 1, PAIRS + 1):
                    v = 1 - u
                    sp.wait_ge(fin2, n)
                    dst = pair_of(out_v, n - 1)
                    sp.dma_start(dst, fin[v][:]).then_inc(stored[v], 16)

            sweep(sp, finish, 0, 2, 16, 17)
            for u in range(2):
                sp.wait_ge(stored[u], 16 * PAIRS // 2)

        @block.tensor
        def _(pe):
            pe.wait_ge(s_cf, 16)
            pe.wait_ge(s_w, 16 * 9)
            pe.wait_ge(bv_done, 1)
            nc.tensor.matmul(bank(0)[:, 0:D], bv_wide[:], w_o[:], start=True, stop=True).then_inc(ball_ps, 1)
            pe.wait_ge(ball_done, 1)
            ident = const("ident")

            def norm(n, u, h):
                if within(n, 0, PAIRS):
                    pe.wait_ge(xn_done, TP * (n + 1))
                    need(pe, xt_done, n - 1)
                    for t in range(TP):
                        ins = nc.tensor.transpose(bank(6 + u)[:, P * t:P * t + P], xn[u][:, t, :], ident)
                    ins.then_inc(xt_ps, 1)
                if within(n, 1, PAIRS + 1):
                    w = 1 - u
                    pe.wait_ge(xt_done, n)
                    need(pe, v_kept, 2 * (n - 1))
                    need(pe, lg_kept, 2 * (n - 1))
                    for t in range(TP):
                        c = t % 2 * (D + NE)
                        ins = nc.tensor.matmul(bank(4 + t // 2)[:, c:c + D + NE], xt[w][:, P * t:P * t + P], w_vr[:],
                                               start=True, stop=True)
                        if t % 2:
                            ins.then_inc(v_ps, 1)
                    for j in range(4):
                        need(pe, rot_done, 4 * (n - 2) + j + 1)
                        nc.tensor.matmul(bank(j), w_qk[:, j, :], xt[w][:], start=True, stop=True).then_inc(proj_ps, 1)

            sweep(pe, norm, 0, 2, 16, 17)

            pe.wait_ge(rot_done, 4 * PAIRS)
            pe.wait_ge(r_hot, 3)
            hot = [parts[k][:, 0, :] for k in range(2)]
            for k in range(2):
                nc.tensor.matmul(bank(k), before[:], hot[k], start=True, stop=True)
                nc.tensor.matmul(bank(2 + k), ones16[:], hot[k], start=True, stop=True).then_inc(r_ps, 1)

            pe.wait_ge(s_init, 16 * 12)
            pe.wait_ge(routed, 1)

            def max_task(n, v, t, loads):
                b_, i, view = task_view(t)
                if t % NCH == 0:
                    pe.wait_ge(qbd_done, 8 * n + 4 * (b_ + 1))
                if t == 0:
                    pe.wait_ge(kr_loaded[v], 48 * loads)
                need(pe, mx_done, 16 * n + t - 1)
                for g in range(G):
                    if i:
                        nc.tensor.matmul(view[:, g, 0:CH * i], qbd[b_][0:KR_ROWS, g, i].rearrange("p h q -> p (h q)"),
                                         kr[v][0:KR_ROWS, g, b_ * T:b_ * T + CH * i], start=True, stop=True)
                    ins = nc.tensor.matmul(view[:, g, CH * i:CH * i + CH], qbd[b_][:, g, i].rearrange("p h q -> p (h q)"),
                                           kr[v][:, g, b_ * T + CH * i:b_ * T + CH * i + CH], start=True, stop=True)
                ins.then_inc(mx_ps, 1)

            def attend(n, u, h):
                w = 1 - u
                loads = h + 1 if u == 0 else h + 2
                main, ahead, behind = within(n, 0, PAIRS), within(n, -1, PAIRS - 1), within(n, 1, PAIRS + 1)
                for k in range(2 * G):
                    b_, g = divmod(k, G)
                    if main:
                        if k == 0:
                            pe.wait_ge(qm_loaded[u], 48 * (h + 1))
                            pe.wait_ge(kp_loaded[u], 192 * (h + 1))
                        if g == 0:
                            pe.wait_ge(m_in[b_], 16 * (n + 1))
                        need(pe, p0_exp, 8 * n + k)
                        for c in range(2):
                            s0 = bank(c).rearrange("p (h t) -> p h t", h=2)[:, :, 0:P]
                            nc.tensor.matmul(s0, big_id[:], cmask[:, None, :].to_broadcast([P, 2, P]),
                                             start=True, stop=False, skip_group_check=True)
                        for hh in range(HG):
                            ins = nc.tensor.matmul(bank(0, 2)[:, T * hh:T * hh + T],
                                                   kp[u][hh][0:M_ROWS, g, b_ * T:b_ * T + P],
                                                   qm[u][0:M_ROWS, g, b_ * T:b_ * T + T], start=False, stop=True, skip_group_check=True)
                        ins.then_inc(s0_ps, 1)
                    if ahead:
                        max_task(n + 1, w, 2 * k, loads)
                    if main:
                        need(pe, p1_exp, 8 * n + k)
                        nc.tensor.matmul(bank(2), big_id[:], cmask[:, None, :].to_broadcast([P, HG, P]),
                                         start=True, stop=False, skip_group_check=True)
                        for hh in range(HG):
                            ins = nc.tensor.matmul(bank(2)[:, P * hh:P * hh + P],
                                                   kp[u][hh][0:M_ROWS, g, b_ * T + P:b_ * T + T],
                                                   qm[u][0:M_ROWS, g, b_ * T + P:b_ * T + T], start=False, stop=True, skip_group_check=True)
                        ins.then_inc(s1_ps, 1)
                    if ahead:
                        max_task(n + 1, w, 2 * k + 1, loads)
                    if (k in (1, 2, 3) and behind) or (k in (5, 6, 7) and main):
                        done = 2 * n - 1 if k < 4 else 2 * n
                        if k % 4 == 1:
                            pe.wait_ge(yu_done, done + 1)
                            need(pe, res_done, done)
                            for s in range(2):
                                for j in range(2):
                                    ins = nc.tensor.transpose(bank(7)[:, P * (2 * j + s):P * (2 * j + s) + P],
                                                              y_u[:, s, P * j:P * j + P], ident)
                            ins.then_inc(ytr_ps, 1)
                        elif k % 4 == 2:
                            pe.wait_ge(yn_done, 4 * (done + 1))
                            for j in range(2):
                                ins = nc.tensor.transpose(bank(7)[:, P * j:P * j + P], y_n[:, j, :], ident)
                            ins.then_inc(yt_ps, 1)
                        else:
                            pe.wait_ge(yt_done, done + 1)
                            for j in range(2):
                                ins = nc.tensor.matmul(bank(7)[:, P * j:P * j + P], y_t[:, P * j:P * j + P], w_o[:],
                                                       start=True, stop=True)
                            ins.then_inc(out_ps, 1)
                    if (k == 0 and behind) or (k > 0 and main):
                        m = 8 * n + k - 1
                        pb, pg = divmod((k - 1) % 8, G)
                        q = (k - 1) % 2
                        pe.wait_ge(p0_exp, m + 1)
                        pe.wait_ge(p1_exp, m + 1)
                        if pg == 0:
                            pe.wait_ge(vp_done[pb], 4 * (n + 1))
                            need(pe, yu_done, 2 * n + pb)
                        s = 0 if pg < 3 else 1
                        for j in range(2):
                            for hh in range(HG):
                                dst = bank(6)[32 * hh:32 * hh + 32, s * T + P * j:(s + 1) * T]
                                src = (p0[q], p1[q])[j][:, hh, :]
                                ins = nc.tensor.matmul(dst, vp[pb][:, j, G * pg + hh, :], src, start=(pg == 0 and j == 0),
                                                       stop=(pg >= 2 and j == 1), skip_group_check=True)
                        ins.then_inc(pv_unit, 1)

            sweep(pe, attend, -1, 1, 13, 17)

            for e in range(NE):
                u = e % 2
                pe.wait_ge(sl_in[u], 16 * (e // 2 + 1))
                if e == 0:
                    pe.wait_ge(res_done, 2 * PAIRS)
                need(pe, st_done, e)
                for t in range(SPE):
                    ins = nc.tensor.transpose(bank(7)[:, P * t:P * t + P], sl[u][:, t, 0:D], ident)
                ins.then_inc(st_ps, 1)
                pe.wait_ge(st_done, e + 1)
                pe.wait_ge(we_in[u], 32 * (e // 2 + 1))
                for c in range(FF // P):
                    need(pe, h_done, 4 * (e - 1) + c + 1)
                    nc.tensor.matmul(bank(c), wi[u][:, P * c:P * c + P], s_t[u][:], start=True, stop=True).then_inc(h_ps, 1)
                need(pe, eo_done, e - 1)
                for t in range(SPE):
                    for c in range(FF // P):
                        if t == 0:
                            pe.wait_ge(h_done, 4 * e + c + 1)
                        ins = nc.tensor.matmul(bank(4 + u)[:, P * t:P * t + P], h_t[u][:, c, P * t:P * t + P],
                                               wo[u][:, P * c:P * c + P], start=(c == 0), stop=(c == FF // P - 1))
                ins.then_inc(eo_ps, 1)

        @block.scalar
        def _(act):
            def norm(n, u, h):
                if within(n, 0, PAIRS):
                    act.wait_ge(mv_done, TP * (n + 1))
                    need(act, rstd_done, n)
                    if isinstance(n, int) and n == 0:
                        act.wait_ge(s_cf, 16)
                    nc.scalar.activation(dev[:], mv[:, :, 1], ACT.Sqrt, bias=const("eps")).then_inc(dev_done, 1)
                    act.wait_ge(xt_ps, n + 1)
                    need(act, v_ps, 2 * (n - 1))
                    need(act, proj_ps, 4 * (n - 1))
                    nc.scalar.copy(xt[u][:], bank(6 + u)).then_inc(xt_done, 1)
                if within(n, 1, PAIRS + 1):
                    for s in range(2):
                        act.wait_ge(v_ps, 2 * (n - 1) + s + 1)
                        src = bank(4 + s)[:, 0:2 * (D + NE)].rearrange("p (t c) -> p t c", t=2)[:, :, 0:D]
                        nc.scalar.copy(v_all[:, bass.ds(n * TP - TP + 2 * s, 2), :], src).then_inc(v_kept, 1)
                if within(n, 2, PAIRS + 2):
                    for s in range(2):
                        act.wait_ge(sum_done, 2 * (n - 2) + s + 1)
                        need(act, parts_stored[u], 16 * (h - 1) if True else 0) if within(n, 4, 99) else None
                        nc.scalar.copy(parts[u][:, 2 * s, :], rot[u][:, 2 * s, :]).then_inc(high_done, 1)

            for n in range(2):
                norm(n, n % 2, n // 2)
            for n in range(2, 4):
                norm(n, n % 2, n // 2)
            with act.Fori(0, 6) as it:
                norm(it * 2 + 4, 0, it + 2)
                norm(it * 2 + 5, 1, it + 2)
            for n in range(16, 18):
                norm(n, n % 2, n // 2)

            e_lg = room(rot[0], 0)
            act.wait_ge(r_dve, 2)
            nc.scalar.activation(e_lg, e_lg, ACT.Exp).then_inc(r_exp, 1)
            act.wait_ge(routed, 1)

            def spread_v(n, b_, j):
                src = v_all[:, bass.ds(n * TP + 2 * b_ + j, 1), :].rearrange("p a (g h d) -> p (a g) h d", g=G, h=HG)
                for g in range(G):
                    off = 9 * g if g < 3 else 0
                    ins = nc.scalar.copy(vp[b_][:, j, G * g:G * g + HG, off:off + DH], src[:, g])
                    if g % 2:
                        ins.then_inc(vp_done[b_], 1)

            def attend(n, u, h):
                main, behind = within(n, 0, PAIRS), within(n, 1, PAIRS + 1)
                if isinstance(n, int) and n == -1:
                    act.wait_ge(s_vones, 1)
                    spread_v(0, 0, 0)
                    spread_v(0, 0, 1)
                for k in range(2 * G):
                    q = k % 2
                    if main:
                        m = 8 * n + k
                        act.wait_ge(s0_ps, m + 1)
                        need(act, pv_unit, m - 1)
                        nc.scalar.activation(p0[q].rearrange("p h t -> p (h t)"), bank(0, 2), ACT.Exp, scale=SCALE).then_inc(p0_exp, 1)
                        act.wait_ge(s1_ps, m + 1)
                        nc.scalar.activation(p1[q].rearrange("p h t -> p (h t)"), bank(2), ACT.Exp, scale=SCALE).then_inc(p1_exp, 1)
                    if (k == 0 and behind) or (k == 4 and main):
                        done = 2 * n - 1 if k < 4 else 2 * n
                        act.wait_ge(pv_unit, 8 * n if k == 0 else 8 * n + 4)
                        need(act, ytr_ps, done)
                        nc.scalar.copy(y_u[:].rearrange("p s t -> p (s t)"), bank(6)).then_inc(yu_done, 1)
                    if k in (1, 2) and main:
                        if k == 1:
                            need(act, pv_unit, 8 * n)
                        spread_v(n, 1, k - 1)
                    if k in (5, 6) and within(n, 0, PAIRS - 1):
                        if k == 5:
                            act.wait_ge(pv_unit, 8 * n + 4)
                        spread_v(n + 1, 0, k - 5)
                    if (k == 2 and behind) or (k == 6 and main):
                        done = 2 * n - 1 if k < 4 else 2 * n
                        act.wait_ge(yt_ps, done + 1)
                        need(act, out_ps, done)
                        nc.scalar.copy(y_t[:], bank(7)[:, 0:T]).then_inc(yt_done, 1)

            sweep(act, attend, -1, 1, 13, 17)

            for e in range(NE):
                u = e % 2
                act.wait_ge(st_ps, e + 1)
                need(act, h_ps, 4 * (e - 1))
                nc.scalar.copy(s_t[u][:], bank(7)).then_inc(st_done, 1)
                for c in range(FF // P):
                    act.wait_ge(h_ps, 4 * e + c + 1)
                    need(act, eo_ps, e - 1)
                    nc.scalar.activation(h_t[u][:, c, :], bank(c), ACT.Gelu_apprx_tanh).then_inc(h_done, 1)

        @block.vector
        def _(dve):
            for i in range(2):
                for hh in range(HG):
                    nc.vector.memset(kp[i][hh][:].bitcast(F32), 0.0).then_inc(s_zero, 1)
            nc.vector.memset(zero_tile[:], 0.0).then_inc(s_zero, 1)
            nc.vector.memset(ones16[:], 1.0).then_inc(s_zero, 1)
            dve.wait_ge(s_w, 16 * 9)
            dve.wait_ge(s_cf, 16)
            dve.wait_ge(s_zero, 10)
            nc.vector.tensor_scalar(bv_wide[:], zero_tile[:, 0:P], b_v[:, 0:1], None, ALU.add).then_inc(bv_done, 1)
            dve.wait_ge(ball_ps, 1)
            nc.vector.tensor_tensor(b_all[:], bank(0)[:, 0:D], b_o[:], ALU.add).then_inc(ball_done, 1)

            tables = [const("rope"), const("rope1"), const("rope"), const("rope1")]

            def rotate(n, u, j):
                dve.wait_ge(proj_ps, 4 * (n - 2) + j + 1)
                if within(n, 4, 99):
                    need(dve, low_done, 2 * (n - 3))
                nc.vector.scalar_tensor_tensor(
                    out=rot[u][:, j, :].rearrange("p (b t) -> p b t", b=2), in0=bank(j).rearrange("p (b t) -> p b t", b=2),
                    scalar=b_qk[:, j:j + 1], in1=tables[j][:, None, :].to_broadcast([P, 2, T]),
                    op0=ALU.add, op1=ALU.mult).then_inc(rot_done, 1)

            def norm(n, u, h):
                if within(n, 0, PAIRS):
                    dve.wait_ge(x_loaded[u], 16 * (h + 1))
                    for t in range(TP):
                        nc.vector.bn_stats(stats[:, t, :], x_in[u][:, t, :]).then_inc(stats_done, 1)
                    for t in range(TP):
                        hold(dve, stats_done, TP * n + t + 1, seen_dve)
                        nc.vector.bn_aggr(mv[:, t, :], stats[:, t, :]).then_inc(mv_done, 1)
                if within(n, 2, PAIRS + 2):
                    for s in range(2):
                        dve.wait_ge(v_ps, 2 * (n - 2) + s + 1)
                        dve.wait_ge(v_kept, 2 * (n - 2) + s + 1)
                        src = bank(4 + s)[:, 0:2 * (D + NE)].rearrange("p (t c) -> p t c", t=2)[:, :, D:D + NE]
                        nc.vector.tensor_copy(lg[:, bass.ds(n * TP - 2 * TP + 2 * s, 2), :], src).then_inc(lg_kept, 1)
                    rotate(n, u, 0)
                    rotate(n, u, 1)
                if within(n, 0, PAIRS):
                    dve.wait_ge(dev_done, n + 1)
                    nc.vector.reciprocal(rstd[:], dev[:]).then_inc(rstd_done, 1)
                    dve.wait_ge(rstd_done, n + 1)
                    if within(n, 2, 99):
                        need(dve, xt_ps, n - 1)
                        dve.wait_ge(xd_copied[u], 16 * h)
                    for t in range(TP):
                        nc.vector.tensor_scalar(xn[u][:, t, :], x_in[u][:, t, :], mv[:, t, 0:1], rstd[:, t:t + 1],
                                                ALU.subtract, ALU.mult).then_inc(xn_done, 1)
                if within(n, 2, PAIRS + 2):
                    rotate(n, u, 2)
                    rotate(n, u, 3)

            for n in range(4):
                norm(n, n % 2, n // 2)
            with dve.Fori(0, 6) as it:
                norm(it * 2 + 4, 0, it + 2)
                norm(it * 2 + 5, 1, it + 2)
            for n in range(16, 18):
                norm(n, n % 2, n // 2)

            steps = [0]

            def after(ins):
                steps[0] += 1
                ins.then_inc(r_dve, 1)
                dve.wait_ge(r_dve, steps[0])

            def wide(t):
                return t.rearrange("p (t e) -> p t e", e=NE)

            def each(t):
                return t[:, :, None].to_broadcast([P, TILES, NE])
            e_lg = room(rot[0], 0)
            tmp = room(rot[0], 1)
            hot32 = [room(rot[0], 2), room(rot[0], 3)]
            cum = [room(rot[1], 0), room(rot[1], 1)]
            tot = [room(rot[1], 2), room(rot[1], 3)]
            small = x_in[0][:].rearrange("p t d -> p (t d)")
            top = [small[:, 0:64], small[:, 64:128]]
            total, place, pos, rank = [small[:, 64 * k:64 * k + 64] for k in range(2, 6)]
            hot16 = [parts[k][:, 0, :] for k in range(2)]

            dve.wait_ge(lg_kept, 2 * PAIRS)
            dve.wait_ge(low_done, 2 * PAIRS)
            dve.wait_ge(xn_done, TP * PAIRS)
            for i in range(2):
                dve.wait_ge(parts_stored[i], 16 * PAIRS // 2)
                dve.wait_ge(xd_copied[i], 16 * PAIRS // 2)
            after(nc.vector.reduce_max(total, lg[:], AX))
            after(nc.vector.tensor_tensor(wide(e_lg), lg[:], each(total), ALU.subtract))
            dve.wait_ge(r_exp, 1)
            after(nc.vector.reduce_sum(total, wide(e_lg), AX))
            after(nc.vector.reciprocal(total, total))
            after(nc.vector.tensor_tensor(wide(e_lg), wide(e_lg), each(total), ALU.mult))
            for k in range(2):
                after(nc.vector.reduce_max(top[k], wide(e_lg), AX))
                after(nc.vector.tensor_tensor(wide(tmp), wide(e_lg), each(top[k]), ALU.is_equal))
                after(nc.vector.tensor_tensor(tmp, tmp, const("order"), ALU.mult))
                after(nc.vector.reduce_max(rank, wide(tmp), AX))
                after(nc.vector.tensor_tensor(wide(hot32[k]), wide(tmp), each(rank), ALU.is_equal))
                nc.vector.tensor_copy(hot16[k], hot32[k]).then_inc(r_hot, 1)
                if k == 0:
                    after(nc.vector.tensor_scalar(xd[:, :, D + 1], rank, -1.0, float(NE), ALU.mult, ALU.add))
                    after(nc.vector.scalar_tensor_tensor(out=e_lg, in0=hot32[0], scalar=-2.0, in1=e_lg, op0=ALU.mult, op1=ALU.add))
                after(nc.vector.tensor_scalar(place, rank, -float(NGRP * CAP), float(NE * NGRP * CAP), ALU.mult, ALU.add))
                after(nc.vector.tensor_tensor((x_in[1][:, k, 0:64]), place, const("grp"), ALU.add))
            nc.vector.tensor_copy(xd[:, :, D], const("tok")).then_inc(r_hot, 1)
            after(nc.vector.tensor_copy(xd[:, :, D + 2], top[0]))
            after(nc.vector.tensor_copy(xd[:, :, D + 3], top[1]))
            dve.wait_ge(r_ps, 2)
            for k in range(2):
                after(nc.vector.tensor_copy(tot[k], bank(2 + k)))
            npt = TILES // NGRP
            tv = [t.rearrange("p (g i e) -> p g i e", g=NGRP, i=npt) for t in tot]
            cv = [c.rearrange("p (g i e) -> p g i e", g=NGRP, i=npt) for c in cum]
            after(nc.vector.memset(cv[0][:, :, 0, :], 0.0))
            for k in range(2):
                if k == 1:
                    after(nc.vector.tensor_tensor(cv[1][:, :, 0, :], cv[0][:, :, npt - 1, :], tv[0][:, :, npt - 1, :], ALU.add))
                for i in range(1, npt):
                    after(nc.vector.tensor_tensor(cv[k][:, :, i, :], cv[k][:, :, i - 1, :], tv[k][:, :, i - 1, :], ALU.add))
            xd_i = xd[:].bitcast(I32)
            for k in range(2):
                after(nc.vector.tensor_tensor(tmp, bank(k), cum[k], ALU.add))
                after(nc.vector.tensor_tensor(tmp, tmp, hot32[k], ALU.mult))
                after(nc.vector.reduce_sum(pos, wide(tmp), AX))
                after(nc.vector.tensor_scalar(rank, pos, float(CAP), NOWHERE, ALU.is_ge, ALU.mult))
                after(nc.vector.tensor_tensor(pos, pos, rank, ALU.add))
                after(nc.vector.tensor_tensor(xd_i[:, :, ROW + k], pos, x_in[1][:, k, 0:64], ALU.add))
            dve.wait_ge(r_hot, 3)
            nc.vector.memset(mx[:], 0.0).then_inc(routed, 1)

            dve.wait_ge(s_init, 16 * 12)
            masks = const("head_rows")

            def spread_q(n, v, b_, hh, h):
                if hh == 0 and b_ == 0:
                    dve.wait_ge(qb_loaded[v], 48 * (h + 1))
                if hh == 0:
                    need(dve, mx_ps, 16 * (n - 1) + 8 * (b_ + 1))
                nc.vector.tensor_scalar(qbd[b_][0:KR_ROWS, :, :, hh, :],
                                        qb[v][0:KR_ROWS, :, b_ * T:b_ * T + T].rearrange("p g (i q) -> p g i q", q=CH),
                                        masks[0:KR_ROWS, hh:hh + 1], None, ALU.mult).then_inc(qbd_done, 1)

            for hh in range(HG):
                spread_q(0, 0, 0, hh, 0)

            def attend(n, u, h):
                w = 1 - u
                main, ahead, behind = within(n, 0, PAIRS), within(n, -1, PAIRS - 1), within(n, 1, PAIRS + 1)
                for k in range(2 * G):
                    if ahead and k < 4:
                        spread_q(n + 1, w, 1, k, None)
                    if k >= 4 and within(n, -1, PAIRS - 2):
                        spread_q(n + 2, u, 0, k - 4, h + 1)
                    if ahead:
                        for t in (2 * k, 2 * k + 1):
                            b_, i, view = task_view(t)
                            dve.wait_ge(mx_ps, 16 * (n + 1) + t + 1)
                            if t % NCH == 0:
                                need(dve, m16_done, 2 * n + b_ + 1)
                            nc.vector.reduce_max(mx[:, b_, :, i], view[:, :, 0:CH * (i + 1)], AX).then_inc(mx_done, 1)
                        if k % 4 == 3:
                            dve.wait_ge(mx_done, 16 * (n + 1) + 8 * (b_ + 1))
                            need(dve, mt_done, 2 * n + b_ + 1)
                            nc.vector.tensor_scalar(mx16[:, b_, :], mx[:, b_].rearrange("p g i -> p (g i)"), -1.0 / MSCALE, None,
                                                    ALU.mult).then_inc(m16_done, 1)
                            dve.wait_ge(m16_done, 2 * (n + 1) + b_ + 1)
                            need(dve, m_out[b_], 16 * (n + 1))
                            nc.vector.transpose(mxt[:, b_, :], mx16[:, b_, :]).then_inc(mt_done, 1)
                    if (k == 1 and behind) or (k == 5 and main):
                        done = 2 * n - 1 if k < 4 else 2 * n
                        dve.wait_ge(ytr_ps, done + 1)
                        need(dve, yt_ps, done)
                        v4 = bank(7).rearrange("p (j s c) -> p j s c", j=2, s=2)
                        for j in range(2):
                            va = v4[:, j, 0, :].rearrange("p (h c) -> p h c", h=HG)[:, :, 0:27].rearrange("p h (g e) -> p h g e", e=9)
                            vb = v4[:, j, 1, :].rearrange("p (h c) -> p h c", h=HG)
                            nc.vector.reciprocal(y_r[:, j, 0, :, :], va[:, :, :, DH]).then_inc(yr_done, 1)
                            nc.vector.reciprocal(y_r[:, j, 1, :, 0], vb[:, :, DH]).then_inc(yr_done, 1)
                        for j in range(2):
                            va = v4[:, j, 0, :].rearrange("p (h c) -> p h c", h=HG)[:, :, 0:27].rearrange("p h (g e) -> p h g e", e=9)
                            vb = v4[:, j, 1, :].rearrange("p (h c) -> p h c", h=HG)
                            yv = y_n[:, j, :].rearrange("p (g h d) -> p h g d", g=G, h=HG)
                            dve.wait_ge(yr_done, 4 * done + 2 * j + 2)
                            nc.vector.tensor_tensor(yv[:, :, 0:3, :], va[:, :, :, 0:DH], y_r[:, j, 0, :, :, None].to_broadcast([P, HG, 3, DH]),
                                                    ALU.mult).then_inc(yn_done, 1)
                            nc.vector.tensor_tensor(yv[:, :, 3, :], vb[:, :, 0:DH], y_r[:, j, 1, :, 0:1].to_broadcast([P, HG, DH]),
                                                    ALU.mult).then_inc(yn_done, 1)
                    if (k == 3 and behind) or (k == 7 and main):
                        done = 2 * n - 1 if k < 4 else 2 * n
                        b_ = 1 if k < 4 else 0
                        dve.wait_ge(out_ps, done + 1)
                        dve.wait_ge(xres_done, n if k < 4 else n + 1)
                        v = w if k < 4 else u
                        if k == 7:
                            dve.wait_ge(stage_in[u], 16 * (h + 1))
                        at_ = n * TP - 2 if k < 4 else n * TP
                        nc.vector.tensor_tensor(xd[:, bass.ds(at_, 2), 0:D], bank(7)[:, 0:T].rearrange("p (j d) -> p j d", j=2),
                                                x_res[v][:, 2 * b_:2 * b_ + 2, :], ALU.add).then_inc(res_done, 1)

            sweep(dve, attend, -1, 1, 13, 17)

            for e in range(NE):
                u = e % 2
                dve.wait_ge(sl_in[u], 16 * (e // 2 + 1))
                need(dve, moe_out[u], 64 * (e // 2))
                first = meta[u][:, :, 0]
                gate = meta[u][:, :, 1]
                nc.vector.tensor_scalar(first, sl[u][:, :, D + 1], float(e), None, ALU.is_equal).then_inc(d_meta, 1)
                nc.vector.tensor_tensor(meta[u][:, :, 2], sl[u][:, :, D + 2], sl[u][:, :, D + 3], ALU.subtract).then_inc(d_meta, 1)
                dve.wait_ge(d_meta, 5 * e + 2)
                nc.vector.tensor_tensor(gate, first, meta[u][:, :, 2], ALU.mult).then_inc(d_meta, 1)
                nc.vector.tensor_scalar(meta[u][:, :, 3], first, -float(NTOK), float(NTOK), ALU.mult, ALU.add).then_inc(d_meta, 1)
                dve.wait_ge(d_meta, 5 * e + 4)
                nc.vector.tensor_tensor(gate, gate, sl[u][:, :, D + 3], ALU.add).then_inc(d_meta, 1)
                nc.vector.tensor_tensor(meta_i[u][:], meta[u][:, :, 3], sl[u][:, :, D], ALU.add).then_inc(idx_done, 1)
                dve.wait_ge(d_meta, 5 * e + 5)
                dve.wait_ge(eo_ps, e + 1)
                nc.vector.tensor_tensor(eo[u][:], bank(4 + u).rearrange("p (t d) -> p t d", t=SPE),
                                        gate[:, :, None].to_broadcast([P, SPE, D]), ALU.mult).then_inc(eo_done, 1)

            def finish(n, u, h):
                dve.wait_ge(acc_in[u], 32 * (h + 1))
                need(dve, stored[u], 16 * h) if within(n, 2, 99) else None
                nc.vector.tensor_tensor(fin[u][:], xd[:, bass.ds(n * TP, TP), 0:D], acc[u][0].rearrange("p (t d) -> p t d", t=TP),
                                        ALU.add).then_inc(fin1, 1)
                dve.wait_ge(fin1, n + 1)
                nc.vector.tensor_tensor(fin[u][:], fin[u][:], acc[u][1].rearrange("p (t d) -> p t d", t=TP), ALU.add).then_inc(fin2, 1)

            sweep(dve, finish, 0, 2, 16, 16)

        @block.gpsimd
        def _(pool):
            nc.gpsimd.memset(slot_fill[:, 0:D], 0.0).then_inc(s_fill, 1)
            nc.gpsimd.memset(slot_fill[:, D:ROW], 2.0 * NTOK).then_inc(s_fill, 1)
            for i in range(2):
                nc.gpsimd.memset(vp[i][:], 0.0).then_inc(s_vzero, 1)
            pool.wait_ge(s_vzero, 2)
            for i in range(2):
                for g in range(G):
                    off = (9 * g if g < 3 else 0) + DH
                    ins = nc.gpsimd.memset(vp[i][:, :, G * g:G * g + HG, off:off + 1], 1.0)
            ins.then_inc(s_vones, 1)

            def norm(n, u, h):
                for s in range(2):
                    pool.wait_ge(rot_done, 4 * (n - 2) + 2 * s + 2)
                    nc.gpsimd.tensor_tensor(rot[u][:, 2 * s, :], rot[u][:, 2 * s, :], rot[u][:, 2 * s + 1, :], ALU.add).then_inc(sum_done, 1)
                for s in range(2):
                    pool.wait_ge(high_done, 2 * (n - 2) + s + 1)
                    nc.gpsimd.tensor_tensor(parts[u][:, 2 * s + 1, :], rot[u][:, 2 * s, :], parts[u][:, 2 * s, :], ALU.subtract).then_inc(low_done, 1)

            sweep(pool, norm, 2, 2, 16, 18)

            pool.wait_ge(ball_done, 1)
            pool.wait_ge(s_slot0, 16 * PAIRS)

            def attend(n, u, h):
                main = within(n, 0, PAIRS)
                if main:
                    pool.wait_ge(xres_in[u], 16 * (h + 1))
                    nc.gpsimd.tensor_tensor(x_res[u], x_res[u], b_all[:, None, :].to_broadcast([P, TP, D]), ALU.add).then_inc(xres_done, 1)
                    hold(pool, stage_in[u], 16 * (h + 1), seen_pool)
                for k in range(2 * G):
                    if main:
                        t, c = divmod(k, 2)
                        nc.gpsimd.indirect_dma_start(
                            slot_dram, bass.IndirectOffsetOnAxis(ap=stage[u][:].bitcast(I32)[:, t, ROW + c:ROW + c + 1], axis=0),
                            stage[u][:, t, 0:ROW], None, bounds_check=SLOTS - 1, oob_is_err=False).then_inc(scattered[u], 16)

            sweep(pool, attend, 0, 2, 16, 16)

            pool.wait_ge(s_moe0, 16 * 2 * PAIRS)
            for e in range(NE):
                u = e % 2
                pool.wait_ge(idx_done, e + 1)
                pool.wait_ge(eo_done, e + 1)
                for t in range(SPE):
                    nc.gpsimd.indirect_dma_start(
                        moe_dram, bass.IndirectOffsetOnAxis(ap=meta_i[u][:, t:t + 1], axis=0),
                        eo[u][:, t, :], None, bounds_check=2 * NTOK - 1, oob_is_err=False).then_inc(moe_out[u], 16)


def kernel(**inputs):
    import concourse.bacc as bacc
    from concourse.bass_utils import run_bass_kernel_spmd as run

    x = np.ascontiguousarray(inputs["L0_attn_x"]).reshape(NTOK, D)
    wqkv = np.asarray(inputs["L0_attn_Wqkv"]).reshape(H, 3, DH, D)
    bqkv = np.asarray(inputs["L0_attn_bqkv"]).reshape(H, 3, DH)
    swap = np.arange(P) ^ 1
    wq, wk, wv = (wqkv[:, k].reshape(P, D) for k in range(3))
    bq, bk, bv = (bqkv[:, k].reshape(P) for k in range(3))
    consts, at = constants()
    arrays = {
        "x": x,
        "w_qk": np.ascontiguousarray(np.stack([wq.T, wq[swap].T, wk.T, wk[swap].T], axis=1)),
        "w_vr": np.ascontiguousarray(np.concatenate([wv.T, np.asarray(inputs["L0_ffn_w_router"])], axis=1)),
        "b_qk": np.ascontiguousarray(np.stack([bq, bq[swap], bk, bk[swap]], axis=1)),
        "b_v": np.ascontiguousarray(bv.reshape(P, 1)),
        "w_o": np.ascontiguousarray(np.asarray(inputs["L0_attn_Wproj"]).T),
        "b_o": np.ascontiguousarray(np.broadcast_to(np.asarray(inputs["L0_attn_bproj"]), (P, D))),
        "wi": np.ascontiguousarray(inputs["L0_ffn_wi"]),
        "wo": np.ascontiguousarray(inputs["L0_ffn_wo"]),
        **consts,
    }
    nc = bacc.Bacc("TRN2", target_bir_lowering=False, num_devices=1)
    args = {n: nc.dram_tensor(n, v.shape, mybir.dt.from_np(v.dtype), kind="ExternalInput").ap() for n, v in arrays.items()}
    args["out"] = nc.dram_tensor("out", (NTOK, D), F32, kind="ExternalOutput").ap()
    attend_and_mix(nc, args, at)
    r = run(nc, [arrays], core_ids=[0])
    return r.results[0]["out"].reshape(B, T, D)
```

```python
from contextlib import ExitStack

import numpy as np

import concourse.bass as bass
from concourse import mybir

F32 = mybir.dt.float32
F16 = mybir.dt.float16
I32 = mybir.dt.int32
ALU = mybir.AluOpType
ACT = mybir.ActivationFunctionType
AX = mybir.AxisListType.X

P = 128
B, T, D, H = 32, 256, 128, 16
DH = D // H
NTOK = B * T
TILES = NTOK // P
PAIRS = B // 2
PT = 2 * T
TP = PT // P
G = 4
HG = H // G
TERMS = 3
KR_ROWS = TERMS * HG * DH
M_ROWS = KR_ROWS + HG
CH = 32
NCH = T // CH
NE, CAP, FF = 8, 64, 512
NGRP = 8
SLOTS = NE * NGRP * CAP
ROW = D + 4
XROW = ROW + 2
COPIES = 4
EPS = 1e-5
SCALE = float(DH) ** -0.5
MSCALE = 256.0
BIG = 32768.0
DUMP = NGRP * CAP
NOWHERE = 1.0e6


def constants():
    pos = np.arange(T, dtype=np.float32)
    ang = pos[:, None] / (np.float32(10000.0) ** (np.arange(0, DH, 2, dtype=np.float32) / np.float32(DH)))
    rope = np.stack([np.cos(ang), np.sin(ang)], axis=-1).reshape(T, DH).astype(np.float32)
    rt = np.tile(rope.T, (H, 1))
    sign = np.where(np.arange(P) % 2 == 0, -1.0, 1.0).astype(np.float32)[:, None]
    rows = np.arange(P)
    f = {}
    f["rope"] = rt
    f["rope1"] = (np.float32(1.0) - rt) * sign
    f["ident"] = np.eye(P, dtype=np.float32)
    f["order"] = np.tile(8.0 - np.arange(NE), (P, TILES))
    f["grp"] = np.tile(np.arange(TILES) // (TILES // NGRP) * CAP, (P, 1))
    f["tok"] = rows[:, None] + P * np.arange(TILES)[None, :]
    f["dump"] = NTOK + rows[:, None] + P * np.arange(DUMP // P)[None, :]
    f["slot_e"] = np.tile(np.arange(SLOTS // P) // (SLOTS // P // NE), (P, 1))
    f["head_rows"] = np.stack([(rows < KR_ROWS) & (rows // DH % HG == hh) for hh in range(HG)], 1)
    f["eps"] = np.full((P, 1), EPS)
    at, parts = {}, []
    n = 0
    for name, a in f.items():
        at[name] = (n, n + a.shape[1])
        n += a.shape[1]
        parts.append(a.astype(np.float32))
    packed = np.concatenate(parts, axis=1)

    before = (rows[:, None] < rows[None, :]).astype(np.float16)
    q, r = np.arange(CH), np.arange(CH)
    kmask = np.where(q[None, :] > r[:, None], -BIG, 0.0)
    return {
        "cf": packed,
        "before": before,
        "cmask": np.where(rows[:, None] > rows[None, :], -BIG, 0.0).astype(np.float16),
        "big_id": (np.eye(P) * BIG).astype(np.float16),
        "kmask": np.tile(kmask, (1, G * PT // CH)).astype(np.float16),
        "qhot": np.tile(np.eye(CH) * BIG, (1, G * NCH * HG)).astype(np.float16),
        "kones": np.stack([np.where(np.arange(HG)[:, None] == hh, MSCALE, 0.0) * np.ones((1, G * PT)) for hh in range(HG)]).astype(np.float16),
    }, at


def sweep(eng, body, start, loop_from, loop_to, end):
    for n in range(start, loop_from):
        body(n, n % 2, n // 2)
    with eng.Fori(0, (loop_to - loop_from) // 2) as it:
        for k in range(2):
            n0 = loop_from + k
            body(it * 2 + n0, n0 % 2, it + n0 // 2)
    for n in range(loop_to, end):
        body(n, n % 2, n // 2)


def within(n, lo, hi):
    return lo <= n < hi if isinstance(n, int) else True


def need(eng, sem, value):
    if not isinstance(value, int) or value > 0:
        eng.wait_ge(sem, value)


def hold(eng, sem, value, seen):
    if not isinstance(value, int):
        eng.wait_ge(sem, value)
        eng.sem_inc(seen, 1)
    elif value > 0:
        eng.wait_ge(sem, value)


def sent_beside(n, u, h):
    if not isinstance(n, int):
        return [(n - 3, 1 - u, h - 1 if u else h - 2)]
    pairs = [n - 3] if 3 <= n < 13 else [2 * n - 16, 2 * n - 15] if 13 <= n < 16 else []
    return [(p, p % 2, p // 2) for p in pairs]


def pair_of(view, n):
    return view[n] if isinstance(n, int) else view[bass.ds(n, 1)].rearrange("a p t d -> p (a t) d")


def attend_and_mix(nc, a, at):
    ctx = ExitStack()
    with ctx:
        def sb(name, shape, dt=F32):
            return ctx.enter_context(nc.sbuf_tensor(name, shape, dt))

        def sem(name):
            return ctx.enter_context(nc.semaphore(name))

        def sem2(name):
            return [sem(f"{name}{i}") for i in range(2)]

        qk_dram = nc.dram_tensor("qk_parts", (PAIRS, 4, P, PT), F16, kind="Internal").ap()
        m_dram = nc.dram_tensor("maxima", (2, 2, P, CH), F16, kind="Internal").ap()
        slot_dram = nc.dram_tensor("slot_rows", (SLOTS, ROW), F32, kind="Internal").ap()
        acc_dram = nc.dram_tensor("sum_rows", (NTOK + DUMP, D), F32, kind="Internal").ap()

        cf = sb("cf_sb", [P, a["cf"].shape[1]])
        def const(name):
            return cf[:, at[name][0]:at[name][1]]
        before = sb("before_sb", [P, P], F16)
        ones16 = sb("ones16", [P, P], F16)
        cmask = sb("cmask_sb", [P, P], F16)
        big_id = sb("big_id_sb", [P, P], F16)
        w_qk = sb("w_qk_sb", [P, 4, P])
        w_vr = sb("w_vr_sb", [P, D + NE])
        w_o = sb("w_o_sb", [P, D])
        b_qk = sb("b_qk_sb", [P, 4])
        b_v = sb("b_v_sb", [P, 1])
        bv_wide = sb("bv_wide", [P, P])
        b_o = sb("b_o_sb", [P, D])
        b_all = sb("b_all", [P, D])

        xd = sb("xd", [P, TILES, XROW])
        v_all = sb("v_all", [P, TILES, D])

        x_in = [sb(f"x_in{i}", [P, TP, D]) for i in range(2)]
        xn = [sb(f"xn{i}", [P, TP, D]) for i in range(2)]
        xt = [sb(f"xt{i}", [P, PT]) for i in range(2)]
        stats = sb("stats", [P, TP, 6])
        mv = sb("mv", [P, TP, 2])
        dev = sb("dev", [P, TP])
        rstd = sb("rstd", [P, TP])
        shift = sb("shift", [P, TP])
        shared = sb("shared", [P, 8 * PT])
        rot = [shared[:, 4 * PT * i:4 * PT * (i + 1)].rearrange("p (j t) -> p j t", j=4) for i in range(2)]
        p0 = [shared[:, HG * T * i:HG * T * (i + 1)].rearrange("p (h t) -> p h t", h=HG) for i in range(2)]
        p1 = [shared[:, 4 * PT + PT * i:4 * PT + PT * (i + 1)].rearrange("p (h t) -> p h t", h=HG) for i in range(2)]
        x_res = [shared[:, 6 * PT + PT * i:6 * PT + PT * (i + 1)].rearrange("p (t d) -> p t d", t=TP) for i in range(2)]
        parts = [sb(f"parts{i}", [P, 4, PT], F16) for i in range(2)]

        qb = [sb(f"qb{i}", [P, G, PT], F16) for i in range(2)]
        kr = [sb(f"kr{i}", [P, G, PT], F16) for i in range(2)]
        qm = [sb(f"qm{i}", [P, G, PT], F16) for i in range(2)]
        kp = [[sb(f"kp{i}{hh}", [P, G, PT], F16) for hh in range(HG)] for i in range(2)]
        qbd = [sb(f"qbd{i}", [P, G, NCH, HG, CH], F16) for i in range(2)]
        mx = sb("mx", [P, 2, G, NCH])
        mx16 = sb("mx16", [P, 2, G * NCH], F16)
        mxt = sb("mxt", [P, 2, CH], F16)
        vp = [sb(f"vp{i}", [P, 2, H, CH]) for i in range(2)]
        y_u = sb("y_u", [P, 2, T])
        y_r = sb("y_r", [P, 2, 2, HG, 3])
        y_n = sb("y_n", [P, 2, D])
        y_t = sb("y_t", [P, T])
        stage = [sb(f"stage{i}", [P, TP, XROW]) for i in range(2)]

        lg = sb("lg", [P, TILES, NE])

        PS = ctx.enter_context(nc.psum_tensor("PS", [P, 8 * 512], F32))

        def bank(k, n=1):
            return PS[:, 512 * k:512 * (k + n)]

        s_cf = sem("const_loaded"); s_w = sem("weights_loaded"); s_init = sem("patterns_loaded")
        s_zero = sem("zeroed"); kp_zero = sem("kp_zeroed"); s_vzero = sem("v_zeroed"); s_vones = sem("v_ones"); s_fill = sem("slot_fill_set"); s_dump0 = sem("dump_rows_zeroed"); s_slot0 = sem("slot_rows_set")
        x_loaded = sem2("x_loaded"); xd_copied = sem2("xd_copied"); parts_stored = sem2("parts_stored")
        stats_done = sem("stats_done"); mv_done = sem("mv_done"); dev_done = sem("dev_done")
        rstd_done = sem("rstd_done"); shift_done = sem("shift_done"); xn_done = sem("xn_done")
        xt_ps = sem("xt_ps"); xt_done = sem("xt_done")
        v_ps = sem("v_ps"); v_kept = sem("v_kept"); lg_kept = sem("lg_kept")
        proj_ps = sem("proj_ps"); rot_done = sem("rot_done"); sum_done = sem("sum_done")
        high_done = sem("high_done"); low_done = sem("low_done")
        bv_done = sem("bv_wide_done"); ball_ps = sem("ball_ps"); ball_done = sem("ball_done")
        r_dve = sem("route_dve"); r_exp = sem("route_exp"); r_hot = sem("route_hot"); r_ps = sem("route_ps")
        r_kept = sem("route_kept"); r_beside = sem("route_beside"); r_pool = sem("route_pool")
        routed = sem("routed")
        seen_sp = sem("seen_sp"); seen_dve = sem("seen_dve"); seen_pool = sem("seen_pool")

        qb_loaded = sem2("qb_loaded"); kr_loaded = sem2("kr_loaded"); qm_loaded = sem2("qm_loaded"); kp_loaded = sem2("kp_loaded")
        m_out = sem2("m_out"); m_in = sem2("m_in"); stage_in = sem2("stage_in"); scattered = sem2("scattered")
        xres_in = sem2("xres_in"); xres_done = sem("xres_done")
        qbd_done = sem("qbd_done"); mx_ps = sem("mx_ps"); mx_done = sem("mx_done"); m16_done = sem("m16_done"); mt_done = sem("mt_done")
        s0_ps = sem("s0_ps"); s1_ps = sem("s1_ps"); p0_exp = sem("p0_exp"); p1_exp = sem("p1_exp")
        pv_unit = sem("pv_unit")
        vp_done = [sem("vp_done0"), sem("vp_done1")]
        yu_done = sem("yu_done"); ytr_ps = sem("ytr_ps"); yr_done = sem("yr_done"); yn_done = sem("yn_done")
        yt_ps = sem("yt_ps"); yt_done = sem("yt_done"); out_ps = sem("out_ps"); res_done = sem("res_done")

        sl_in = sem2("sl_in"); we_in = sem2("we_in"); d_meta = sem("d_meta"); idx_done = sem("idx_done")
        st_ps = sem("st_ps"); st_done = sem("st_done"); h_ps = sem("h_ps"); h_done = sem("h_done")
        eo_ps = sem("eo_ps"); eo_done = sem("eo_done"); moe_out = sem2("moe_out")
        sum_stored = sem2("sum_stored"); out_stored = sem("out_stored")

        x_v = a["x"].rearrange("(n t p) d -> n p t d", t=TP, p=P)
        acc_v = acc_dram[0:NTOK].rearrange("(n t p) d -> n p t d", t=TP, p=P)

        SPE = SLOTS // NE // P
        sl = [stage[i] for i in range(2)]
        wi = [qb[i][:, 0:2, :].bitcast(F32).rearrange("p g t -> p (g t)") for i in range(2)]
        wo = [qb[i][:, 2:4, :].bitcast(F32).rearrange("p g t -> p (g t)") for i in range(2)]
        s_t = [xt[i] for i in range(2)]
        h_t = [rot[i] for i in range(2)]
        eo = [xn[i] for i in range(2)]
        meta = [sb(f"meta{i}", [P, SPE, 3]) for i in range(2)]
        meta_i = [sb(f"meta_i{i}", [P, SPE], I32) for i in range(2)]

        zero_tile = sb("zero_tile", [P, PT])
        slot_fill = sb("slot_fill", [P, ROW])

        def wide(t):
            return t.rearrange("p (t e) -> p t e", e=NE)

        def each(t):
            return t[:, :, None].to_broadcast([P, TILES, NE])
        e_lg, tmp = [x_in[k][:].rearrange("p t d -> p (t d)") for k in range(2)]
        hot32 = [xn[k][:].rearrange("p t d -> p (t d)") for k in range(2)]
        hot16 = [lg[:].bitcast(F16).rearrange("p t e -> p (t e)")[:, PT * k:PT * k + PT] for k in range(2)]
        queued = [xt[k][:] for k in range(2)]
        tile_room = [parts[k][:].bitcast(F32).rearrange("p j t -> p (j t)") for k in range(2)]
        ahead_in_tile = [tile_room[k][:, 0:PT] for k in range(2)]
        tile_total = [tile_room[k][:, PT:2 * PT] for k in range(2)]
        total, top0, top1, rank0, rank1, place, pos, over = [zero_tile[:, TILES * k:TILES * k + TILES] for k in range(8)]
        top, rank = [top0, top1], [rank0, rank1]

        block = ctx.enter_context(nc.Block())

        def task_view(t):
            b_, c = divmod(t, NCH)
            i = NCH - 1 - c // 2 if c % 2 == 0 else NCH // 2 - 1 - c // 2
            if i >= NCH // 2:
                return b_, i, bank(3, 2).rearrange("p (g t) -> p g t", g=G)
            return b_, i, bank(5).rearrange("p (g t) -> p g t", g=G)

        @block.sync
        def _(sp):
            sp.dma_start(x_in[0][:], x_v[0]).then_inc(x_loaded[0], 16)
            sp.dma_start(cf[:], a["cf"]).then_inc(s_cf, 16)
            sp.dma_start(w_qk[:], a["w_qk"]).then_inc(s_w, 16)
            sp.dma_start(w_vr[:], a["w_vr"]).then_inc(s_w, 16)
            sp.dma_start(b_qk[:], a["b_qk"]).then_inc(s_w, 16)
            sp.dma_start(b_v[:], a["b_v"]).then_inc(s_w, 16)
            sp.dma_start(w_o[:], a["w_o"]).then_inc(s_w, 16)
            sp.dma_start(b_o[:], a["b_o"]).then_inc(s_w, 16)
            sp.dma_start(before[:], a["before"]).then_inc(s_w, 16)
            sp.dma_start(cmask[:], a["cmask"]).then_inc(s_w, 16)
            sp.dma_start(big_id[:], a["big_id"]).then_inc(s_w, 16)

            sp.dma_start(x_in[1][:], x_v[1]).then_inc(x_loaded[1], 16)
            sp.wait_ge(s_zero, 2)
            sp.wait_ge(s_fill, 2)
            sp.dma_start(acc_dram[NTOK:].rearrange("(t p) d -> p t d", p=P),
                         zero_tile[:].rearrange("p (t d) -> p t d", d=D)).then_inc(s_dump0, 16)
            slot_v = slot_dram.rearrange("(n t p) d -> n p t d", n=PAIRS, p=P)

            def norm(n, u, h):
                if within(n, 1, PAIRS - 1):
                    need(sp, xn_done, n * TP)
                    sp.dma_start(x_in[1 - u][:], pair_of(x_v, n + 1)).then_inc(x_loaded[1 - u], 16)
                if within(n, 0, PAIRS):
                    fill = slot_fill[:, None, :].to_broadcast([P, SLOTS // P // PAIRS, ROW])
                    sp.dma_start(pair_of(slot_v, n), fill).then_inc(s_slot0, 16)
                if within(n, 1, PAIRS + 1):
                    v = 1 - u
                    sp.wait_ge(xn_done, n * TP)
                    sp.dma_start(xd[:, bass.ds(n * TP - TP, TP), 0:D], xn[v][:]).then_inc(xd_copied[v], 16)
                if within(n, 3, PAIRS + 3):
                    v = 1 - u
                    sp.wait_ge(low_done, 2 * (n - 2))
                    sp.dma_start(qk_dram[bass.ds(n - 3, 1)].rearrange("a x p t -> p (a x) t"),
                                 parts[v][:]).then_inc(parts_stored[v], 16)

            for n in range(3):
                norm(n, n % 2, n // 2)
            with sp.Fori(0, 6) as it:
                norm(it * 2 + 3, 1, it + 1)
                norm(it * 2 + 4, 0, it + 2)
            sp.wait_ge(kp_zero, 8)
            for i in range(2):
                sp.dma_start(kr[i][KR_ROWS:P, :, :].rearrange("p g t -> p (g t)"), a["kmask"]).then_inc(s_init, 16)
                sp.dma_start(qbd[i][KR_ROWS:P].rearrange("p g i h q -> p (g i h q)"), a["qhot"]).then_inc(s_init, 16)
                for hh in range(HG):
                    sp.dma_start(kp[i][hh][KR_ROWS:M_ROWS].rearrange("p g t -> p (g t)"), a["kones"][hh]).then_inc(s_init, 16)

            def part_rows(pair, part):
                return qk_dram[pair, part].rearrange("(g r) t -> r g t", g=G) if isinstance(pair, int) else \
                    qk_dram[bass.ds(pair, 1), part].rearrange("a (g r) t -> r (a g) t", g=G)

            Q_HI, Q_LO, K_HI, K_LO = range(4)

            def load_max_operands(n, v):
                for term, part in enumerate((Q_HI, Q_HI, Q_LO)):
                    sp.dma_start(qb[v][32 * term:32 * term + 32], part_rows(n, part)).then_inc(qb_loaded[v], 16)
                for term, part in enumerate((K_HI, K_LO, K_HI)):
                    sp.dma_start(kr[v][32 * term:32 * term + 32], part_rows(n, part)).then_inc(kr_loaded[v], 16)

            def load_main_operands(n, v):
                for term, part in enumerate((Q_HI, Q_HI, Q_LO)):
                    sp.dma_start(qm[v][32 * term:32 * term + 32], part_rows(n, part)).then_inc(qm_loaded[v], 16)
                for term, part in enumerate((K_HI, K_LO, K_HI)):
                    for hh in range(HG):
                        r0 = 32 * term + DH * hh
                        src = part_rows(n, part)[DH * hh:DH * hh + DH]
                        sp.dma_start(kp[v][hh][r0:r0 + DH], src).then_inc(kp_loaded[v], 16)

            sp.wait_ge(s_init, 16 * 12)
            norm(15, 1, 7)
            sp.wait_ge(parts_stored[0], 16)
            load_max_operands(0, 0)
            norm(16, 0, 8)
            sp.wait_ge(parts_stored[1], 16)
            load_max_operands(1, 1)
            norm(17, 1, 8)
            load_main_operands(0, 0)
            norm(18, 0, 9)
            sp.wait_ge(parts_stored[0], 16 * PAIRS // 2)
            sp.wait_ge(parts_stored[1], 16 * PAIRS // 2)

            def attend(n, u, h):
                w = 1 - u
                if within(n, 0, PAIRS - 2):
                    hold(sp, qbd_done, 8 * (n + 1), seen_sp)
                    hold(sp, mx_ps, 16 * (n + 1), seen_sp)
                    load_max_operands(n + 2, u)
                if within(n, 0, PAIRS):
                    need(sp, sum_stored[u], 16 * h)
                    sp.dma_start(x_res[u], pair_of(x_v, n)).then_inc(xres_in[u], 16)
                for pair, v, hp in sent_beside(n, u, h):
                    if isinstance(n, int) and pair == 0:
                        sp.wait_ge(routed, 1)
                    need(sp, scattered[v], 128 * hp)
                    sp.dma_start(stage[v][:], xd[:, bass.ds(pair * TP, TP), :]).then_inc(stage_in[v], 16)
                if within(n, 0, PAIRS - 1):
                    need(sp, s1_ps, 8 * n)
                    load_main_operands(n + 1, w)
                if within(n, -1, PAIRS - 1):
                    for b_ in range(2):
                        sp.wait_ge(mt_done, 2 * (n + 1) + b_ + 1)
                        sp.dma_start(m_dram[w, b_], mxt[:, b_, :]).then_inc(m_out[b_], 16)
                        sp.wait_ge(m_out[b_], 16 * (n + 2))
                        sp.dma_start(qm[w][KR_ROWS:M_ROWS, :, b_ * T:(b_ + 1) * T],
                                     m_dram[w, b_].rearrange("(r g i) q -> r g (i q)", r=HG, g=G)).then_inc(m_in[b_], 16)
                if within(n, 1, PAIRS + 1):
                    sp.wait_ge(res_done, 2 * n)
                    sp.dma_start(pair_of(acc_v, n - 1), x_res[w]).then_inc(sum_stored[w], 16)

            sweep(sp, attend, -1, 5, 13, 17)

            def expert(e):
                u = e % 2
                if e == 0:
                    sp.wait_ge(scattered[0], 128 * PAIRS // 2)
                    sp.wait_ge(scattered[1], 128 * PAIRS // 2)
                    sp.wait_ge(res_done, 2 * PAIRS)
                if e >= 2:
                    sp.wait_ge(eo_ps, e - 1)
                    sp.wait_ge(eo_done, e - 1)
                sp.dma_start(sl[u][:, :, 0:ROW], slot_dram[e * SPE * P:(e + 1) * SPE * P, :]
                             .rearrange("(t p) d -> p t d", p=P)).then_inc(sl_in[u], 16)
                sp.dma_start(wi[u], a["wi"][e]).then_inc(we_in[u], 16)
                sp.dma_start(wo[u].rearrange("p (c d) -> p c d", c=FF // P), a["wo"][e].rearrange("(c p) d -> p c d", p=P)).then_inc(we_in[u], 16)

            for e in range(NE):
                expert(e)

            sp.wait_ge(moe_out[0], 64 * NE // 2)
            sp.wait_ge(moe_out[1], 64 * NE // 2)
            for n in range(COPIES):
                rows = slice(n * NTOK // COPIES, (n + 1) * NTOK // COPIES)
                sp.dma_start(a["out"][rows], acc_dram[rows]).then_inc(out_stored, 16)
            sp.wait_ge(out_stored, 16 * COPIES)

        @block.tensor
        def _(pe):
            pe.wait_ge(s_cf, 16)
            pe.wait_ge(s_w, 16 * 9)
            pe.wait_ge(bv_done, 1)
            nc.tensor.matmul(bank(0)[:, 0:D], bv_wide[:], w_o[:], start=True, stop=True).then_inc(ball_ps, 1)
            pe.wait_ge(ball_done, 1)
            ident = const("ident")

            def norm(n, u, h):
                w = 1 - u
                if within(n, 1, PAIRS + 1):
                    pe.wait_ge(xt_done, n)
                    need(pe, v_kept, 2 * (n - 1))
                    need(pe, lg_kept, 2 * (n - 1))
                    for t in range(TP):
                        c = t % 2 * (D + NE)
                        ins = nc.tensor.matmul(bank(4 + t // 2)[:, c:c + D + NE], xt[w][:, P * t:P * t + P], w_vr[:],
                                               start=True, stop=True)
                        if t % 2:
                            ins.then_inc(v_ps, 1)
                    for j in range(2):
                        need(pe, rot_done, 4 * (n - 2) + j + 1)
                        nc.tensor.matmul(bank(j), w_qk[:, j, :], xt[w][:], start=True, stop=True).then_inc(proj_ps, 1)
                if within(n, 0, PAIRS):
                    pe.wait_ge(xn_done, TP * (n + 1))
                    need(pe, xt_done, n - 1)
                    for t in range(TP):
                        ins = nc.tensor.transpose(bank(6 + u)[:, P * t:P * t + P], xn[u][:, t, :], ident)
                    ins.then_inc(xt_ps, 1)
                if within(n, 1, PAIRS + 1):
                    for j in range(2, 4):
                        need(pe, rot_done, 4 * (n - 2) + j + 1)
                        nc.tensor.matmul(bank(j), w_qk[:, j, :], xt[w][:], start=True, stop=True).then_inc(proj_ps, 1)

            sweep(pe, norm, 0, 2, 16, 17)

            pe.wait_ge(s_init, 16 * 12)
            pe.wait_ge(rot_done, 4 * PAIRS)
            pe.wait_ge(v_kept, 2 * PAIRS)
            pe.wait_ge(lg_kept, 2 * PAIRS)
            pe.wait_ge(xt_done, PAIRS)

            def queues():
                pe.wait_ge(r_hot, 2)
                pe.wait_ge(p0_exp, 16)
                pe.wait_ge(p1_exp, 16)
                pe.wait_ge(res_done, 3)
                for i in range(2):
                    nc.tensor.matmul(bank(i), before[:], hot16[i], start=True, stop=True)
                    nc.tensor.matmul(bank((2, 7)[i]), ones16[:], hot16[i], start=True, stop=True).then_inc(r_ps, 1)
                pe.wait_ge(r_kept, 4)

            def max_task(n, v, t, loads):
                b_, i, view = task_view(t)
                if t % NCH == 0:
                    pe.wait_ge(qbd_done, 8 * n + 4 * (b_ + 1))
                if t == 0:
                    pe.wait_ge(kr_loaded[v], 48 * loads)
                need(pe, mx_done, 16 * n + t - 1)
                for g in range(G):
                    if i:
                        nc.tensor.matmul(view[:, g, 0:CH * i], qbd[b_][0:KR_ROWS, g, i].rearrange("p h q -> p (h q)"),
                                         kr[v][0:KR_ROWS, g, b_ * T:b_ * T + CH * i], start=True, stop=True)
                    ins = nc.tensor.matmul(view[:, g, CH * i:CH * i + CH], qbd[b_][:, g, i].rearrange("p h q -> p (h q)"),
                                           kr[v][:, g, b_ * T + CH * i:b_ * T + CH * i + CH], start=True, stop=True)
                ins.then_inc(mx_ps, 1)

            def attend(n, u, h):
                w = 1 - u
                loads = h + 1 if u == 0 else h + 2
                main, ahead, behind = within(n, 0, PAIRS), within(n, -1, PAIRS - 1), within(n, 1, PAIRS + 1)
                for k in range(2 * G):
                    b_, g = divmod(k, G)
                    if isinstance(n, int) and (n, k) == (2, 0):
                        queues()
                    if main:
                        if k == 0:
                            pe.wait_ge(qm_loaded[u], 48 * (h + 1))
                            pe.wait_ge(kp_loaded[u], 192 * (h + 1))
                        if g == 0:
                            pe.wait_ge(m_in[b_], 16 * (n + 1))
                        need(pe, p0_exp, 8 * n + k)
                        for c in range(2):
                            s0 = bank(c).rearrange("p (h t) -> p h t", h=2)[:, :, 0:P]
                            nc.tensor.matmul(s0, big_id[:], cmask[:, None, :].to_broadcast([P, 2, P]),
                                             start=True, stop=False, skip_group_check=True)
                        for hh in range(HG):
                            ins = nc.tensor.matmul(bank(0, 2)[:, T * hh:T * hh + T],
                                                   kp[u][hh][0:M_ROWS, g, b_ * T:b_ * T + P],
                                                   qm[u][0:M_ROWS, g, b_ * T:b_ * T + T], start=False, stop=True, skip_group_check=True)
                        ins.then_inc(s0_ps, 1)
                    if ahead:
                        max_task(n + 1, w, 2 * k, loads)
                    if main:
                        need(pe, p1_exp, 8 * n + k)
                        nc.tensor.matmul(bank(2), big_id[:], cmask[:, None, :].to_broadcast([P, HG, P]),
                                         start=True, stop=False, skip_group_check=True)
                        for hh in range(HG):
                            ins = nc.tensor.matmul(bank(2)[:, P * hh:P * hh + P],
                                                   kp[u][hh][0:M_ROWS, g, b_ * T + P:b_ * T + T],
                                                   qm[u][0:M_ROWS, g, b_ * T + P:b_ * T + T], start=False, stop=True, skip_group_check=True)
                        ins.then_inc(s1_ps, 1)
                    if ahead:
                        max_task(n + 1, w, 2 * k + 1, loads)
                    if (k in (1, 2, 3) and behind) or (k in (5, 6, 7) and main):
                        done = 2 * n - 1 if k < 4 else 2 * n
                        if k % 4 == 1:
                            pe.wait_ge(yu_done, done + 1)
                            need(pe, res_done, done)
                            for s in range(2):
                                for j in range(2):
                                    ins = nc.tensor.transpose(bank(7)[:, P * (2 * j + s):P * (2 * j + s) + P],
                                                              y_u[:, s, P * j:P * j + P], ident)
                            ins.then_inc(ytr_ps, 1)
                        elif k % 4 == 2:
                            pe.wait_ge(yn_done, 4 * (done + 1))
                            for j in range(2):
                                ins = nc.tensor.transpose(bank(7)[:, P * j:P * j + P], y_n[:, j, :], ident)
                            ins.then_inc(yt_ps, 1)
                        else:
                            pe.wait_ge(yt_done, done + 1)
                            for j in range(2):
                                ins = nc.tensor.matmul(bank(7)[:, P * j:P * j + P], y_t[:, P * j:P * j + P], w_o[:],
                                                       start=True, stop=True)
                            ins.then_inc(out_ps, 1)
                    if (k == 0 and behind) or (k > 0 and main):
                        m = 8 * n + k - 1
                        pb, pg = divmod((k - 1) % 8, G)
                        q = (k - 1) % 2
                        pe.wait_ge(p0_exp, m + 1)
                        pe.wait_ge(p1_exp, m + 1)
                        if pg == 0:
                            pe.wait_ge(vp_done[pb], 4 * (n + 1))
                            need(pe, yu_done, 2 * n + pb)
                        s = 0 if pg < 3 else 1
                        for j in range(2):
                            for hh in range(HG):
                                dst = bank(6)[32 * hh:32 * hh + 32, s * T + P * j:(s + 1) * T]
                                src = (p0[q], p1[q])[j][:, hh, :]
                                ins = nc.tensor.matmul(dst, vp[pb][:, j, G * pg + hh, :], src, start=(pg == 0 and j == 0),
                                                       stop=(pg >= 2 and j == 1), skip_group_check=True)
                        ins.then_inc(pv_unit, 1)

            sweep(pe, attend, -1, 3, 13, 17)

            for e in range(NE):
                u = e % 2
                pe.wait_ge(sl_in[u], 16 * (e // 2 + 1))
                if e == 0:
                    pe.wait_ge(res_done, 2 * PAIRS)
                need(pe, st_done, e)
                for t in range(SPE):
                    ins = nc.tensor.transpose(bank(7)[:, P * t:P * t + P], sl[u][:, t, 0:D], ident)
                ins.then_inc(st_ps, 1)
                pe.wait_ge(st_done, e + 1)
                pe.wait_ge(we_in[u], 32 * (e // 2 + 1))
                for c in range(FF // P):
                    need(pe, h_done, 4 * (e - 1) + c + 1)
                    nc.tensor.matmul(bank(c), wi[u][:, P * c:P * c + P], s_t[u][:], start=True, stop=True).then_inc(h_ps, 1)
                need(pe, eo_done, e - 1)
                for t in range(SPE):
                    for c in range(FF // P):
                        if t == 0:
                            pe.wait_ge(h_done, 4 * e + c + 1)
                        ins = nc.tensor.matmul(bank(4 + u)[:, P * t:P * t + P], h_t[u][:, c, P * t:P * t + P],
                                               wo[u][:, P * c:P * c + P], start=(c == 0), stop=(c == FF // P - 1))
                ins.then_inc(eo_ps, 1)

        @block.scalar
        def _(act):
            def norm(n, u, h):
                if within(n, 0, PAIRS):
                    act.wait_ge(mv_done, TP * (n + 1))
                    need(act, rstd_done, n)
                    if isinstance(n, int) and n == 0:
                        act.wait_ge(s_cf, 16)
                    nc.scalar.activation(dev[:], mv[:, :, 1], ACT.Sqrt, bias=const("eps")).then_inc(dev_done, 1)
                if within(n, 1, PAIRS + 1):
                    for s in range(2):
                        act.wait_ge(v_ps, 2 * (n - 1) + s + 1)
                        src = bank(4 + s)[:, 0:2 * (D + NE)].rearrange("p (t c) -> p t c", t=2)[:, :, 0:D]
                        nc.scalar.copy(v_all[:, bass.ds(n * TP - TP + 2 * s, 2), :], src).then_inc(v_kept, 1)
                if within(n, 0, PAIRS):
                    act.wait_ge(shift_done, n + 1)
                    if within(n, 2, 99):
                        need(act, xt_ps, n - 1)
                        act.wait_ge(xd_copied[u], 16 * h)
                    for t in range(TP):
                        nc.scalar.activation(xn[u][:, t, :], x_in[u][:, t, :], ACT.Identity, bias=shift[:, t:t + 1],
                                             scale=rstd[:, t:t + 1]).then_inc(xn_done, 1)
                    act.wait_ge(xt_ps, n + 1)
                    need(act, v_ps, 2 * (n - 1))
                    need(act, proj_ps, 4 * (n - 1))
                    nc.scalar.copy(xt[u][:], bank(6 + u)).then_inc(xt_done, 1)
                if within(n, 2, PAIRS + 2):
                    for s in range(2):
                        act.wait_ge(sum_done, 2 * (n - 2) + s + 1)
                        need(act, parts_stored[u], 16 * (h - 1) if True else 0) if within(n, 4, 99) else None
                        nc.scalar.copy(parts[u][:, 2 * s, :], rot[u][:, 2 * s, :]).then_inc(high_done, 1)

            for n in range(2):
                norm(n, n % 2, n // 2)
            for n in range(2, 4):
                norm(n, n % 2, n // 2)
            with act.Fori(0, 6) as it:
                norm(it * 2 + 4, 0, it + 2)
                norm(it * 2 + 5, 1, it + 2)
            for n in range(16, 18):
                norm(n, n % 2, n // 2)

            act.wait_ge(low_done, 2 * PAIRS)

            def spread_v(n, b_, j):
                src = v_all[:, bass.ds(n * TP + 2 * b_ + j, 1), :].rearrange("p a (g h d) -> p (a g) h d", g=G, h=HG)
                for g in range(G):
                    off = 9 * g if g < 3 else 0
                    ins = nc.scalar.copy(vp[b_][:, j, G * g:G * g + HG, off:off + DH], src[:, g])
                    if g % 2:
                        ins.then_inc(vp_done[b_], 1)

            def attend(n, u, h):
                main, behind = within(n, 0, PAIRS), within(n, 1, PAIRS + 1)
                if isinstance(n, int) and n == -1:
                    act.wait_ge(s_vones, 1)
                    spread_v(0, 0, 0)
                    spread_v(0, 0, 1)
                for k in range(2 * G):
                    q = k % 2
                    if isinstance(n, int) and (n, k) == (0, 1):
                        act.wait_ge(r_dve, 2)
                        nc.scalar.activation(e_lg, e_lg, ACT.Exp).then_inc(r_exp, 1)
                    if isinstance(n, int) and (n, k) == (2, 0):
                        for i in range(2):
                            act.wait_ge(parts_stored[i], 16 * PAIRS // 2)
                        act.wait_ge(r_ps, 2)
                        for i in range(2):
                            nc.scalar.copy(ahead_in_tile[i], bank(i)).then_inc(r_kept, 1)
                            nc.scalar.copy(tile_total[i], bank((2, 7)[i])).then_inc(r_kept, 1)
                    if main:
                        m = 8 * n + k
                        act.wait_ge(s0_ps, m + 1)
                        need(act, pv_unit, m - 1)
                        nc.scalar.activation(p0[q].rearrange("p h t -> p (h t)"), bank(0, 2), ACT.Exp, scale=SCALE).then_inc(p0_exp, 1)
                        act.wait_ge(s1_ps, m + 1)
                        nc.scalar.activation(p1[q].rearrange("p h t -> p (h t)"), bank(2), ACT.Exp, scale=SCALE).then_inc(p1_exp, 1)
                    if (k == 0 and behind) or (k == 4 and main):
                        done = 2 * n - 1 if k < 4 else 2 * n
                        act.wait_ge(pv_unit, 8 * n if k == 0 else 8 * n + 4)
                        need(act, ytr_ps, done)
                        nc.scalar.copy(y_u[:].rearrange("p s t -> p (s t)"), bank(6)).then_inc(yu_done, 1)
                    if k in (1, 2) and main:
                        if k == 1:
                            need(act, pv_unit, 8 * n)
                        spread_v(n, 1, k - 1)
                    if k in (5, 6) and within(n, 0, PAIRS - 1):
                        if k == 5:
                            act.wait_ge(pv_unit, 8 * n + 4)
                        spread_v(n + 1, 0, k - 5)
                    if (k == 2 and behind) or (k == 6 and main):
                        done = 2 * n - 1 if k < 4 else 2 * n
                        act.wait_ge(yt_ps, done + 1)
                        need(act, out_ps, done)
                        nc.scalar.copy(y_t[:], bank(7)[:, 0:T]).then_inc(yt_done, 1)

            sweep(act, attend, -1, 3, 13, 17)

            for e in range(NE):
                u = e % 2
                act.wait_ge(st_ps, e + 1)
                need(act, h_ps, 4 * (e - 1))
                nc.scalar.copy(s_t[u][:], bank(7)).then_inc(st_done, 1)
                for c in range(FF // P):
                    act.wait_ge(h_ps, 4 * e + c + 1)
                    need(act, eo_ps, e - 1)
                    nc.scalar.activation(h_t[u][:, c, :], bank(c), ACT.Gelu_apprx_tanh).then_inc(h_done, 1)

        @block.vector
        def _(dve):
            nc.vector.memset(zero_tile[:], 0.0).then_inc(s_zero, 1)
            nc.vector.memset(ones16[:], 1.0).then_inc(s_zero, 1)
            dve.wait_ge(s_w, 16 * 9)
            dve.wait_ge(s_cf, 16)
            dve.wait_ge(s_zero, 2)
            nc.vector.tensor_scalar(bv_wide[:], zero_tile[:, 0:P], b_v[:, 0:1], None, ALU.add).then_inc(bv_done, 1)
            dve.wait_ge(ball_ps, 1)
            nc.vector.tensor_tensor(b_all[:], bank(0)[:, 0:D], b_o[:], ALU.add).then_inc(ball_done, 1)

            tables = [const("rope"), const("rope1"), const("rope"), const("rope1")]

            def rotate(n, u, j):
                dve.wait_ge(proj_ps, 4 * (n - 2) + j + 1)
                if within(n, 4, 99):
                    need(dve, low_done, 2 * (n - 3))
                nc.vector.scalar_tensor_tensor(
                    out=rot[u][:, j, :].rearrange("p (b t) -> p b t", b=2), in0=bank(j).rearrange("p (b t) -> p b t", b=2),
                    scalar=b_qk[:, j:j + 1], in1=tables[j][:, None, :].to_broadcast([P, 2, T]),
                    op0=ALU.add, op1=ALU.mult).then_inc(rot_done, 1)

            def norm(n, u, h):
                if within(n, 2, PAIRS + 2):
                    for s in range(2):
                        dve.wait_ge(v_ps, 2 * (n - 2) + s + 1)
                        dve.wait_ge(v_kept, 2 * (n - 2) + s + 1)
                        src = bank(4 + s)[:, 0:2 * (D + NE)].rearrange("p (t c) -> p t c", t=2)[:, :, D:D + NE]
                        nc.vector.tensor_copy(lg[:, bass.ds(n * TP - 2 * TP + 2 * s, 2), :], src).then_inc(lg_kept, 1)
                if within(n, 0, PAIRS):
                    dve.wait_ge(x_loaded[u], 16 * (h + 1))
                    for t in range(TP):
                        nc.vector.bn_stats(stats[:, t, :], x_in[u][:, t, :]).then_inc(stats_done, 1)
                    for t in range(TP):
                        hold(dve, stats_done, TP * n + t + 1, seen_dve)
                        nc.vector.bn_aggr(mv[:, t, :], stats[:, t, :]).then_inc(mv_done, 1)
                if within(n, 2, PAIRS + 2):
                    rotate(n, u, 0)
                if within(n, 0, PAIRS):
                    dve.wait_ge(dev_done, n + 1)
                    need(dve, xn_done, TP * n)
                    nc.vector.reciprocal(rstd[:], dev[:]).then_inc(rstd_done, 1)
                    dve.wait_ge(rstd_done, n + 1)
                    nc.vector.scalar_tensor_tensor(out=shift[:], in0=mv[:, :, 0], scalar=-1.0, in1=rstd[:],
                                                   op0=ALU.mult, op1=ALU.mult).then_inc(shift_done, 1)
                if within(n, 2, PAIRS + 2):
                    rotate(n, u, 1)
                    rotate(n, u, 2)
                    rotate(n, u, 3)

            for n in range(4):
                norm(n, n % 2, n // 2)
            with dve.Fori(0, 6) as it:
                norm(it * 2 + 4, 0, it + 2)
                norm(it * 2 + 5, 1, it + 2)
            for n in range(16, 18):
                norm(n, n % 2, n // 2)

            dve.wait_ge(s_init, 16 * 12)
            masks = const("head_rows")

            def spread_q(n, v, b_, hh, h):
                if hh == 0 and b_ == 0:
                    dve.wait_ge(qb_loaded[v], 48 * (h + 1))
                if hh == 0:
                    need(dve, mx_ps, 16 * (n - 1) + 8 * (b_ + 1))
                nc.vector.tensor_scalar(qbd[b_][0:KR_ROWS, :, :, hh, :],
                                        qb[v][0:KR_ROWS, :, b_ * T:b_ * T + T].rearrange("p g (i q) -> p g i q", q=CH),
                                        masks[0:KR_ROWS, hh:hh + 1], None, ALU.mult).then_inc(qbd_done, 1)

            for hh in range(HG):
                spread_q(0, 0, 0, hh, 0)

            steps = [0]

            def last_step():
                if steps[0]:
                    dve.wait_ge(r_dve, steps[0])

            def counted(ins):
                steps[0] += 1
                ins.then_inc(r_dve, 1)

            def mark(k):
                last_step()
                counted(nc.vector.tensor_tensor(wide(tmp), wide(e_lg), each(top[k]), ALU.is_equal))

            def order(k):
                last_step()
                counted(nc.vector.tensor_tensor(tmp, tmp, const("order"), ALU.mult))

            def first_marked(k):
                last_step()
                counted(nc.vector.reduce_max(rank[k], wide(tmp), AX))

            def one_hot(k):
                last_step()
                counted(nc.vector.tensor_tensor(wide(hot32[k]), wide(tmp), each(rank[k]), ALU.is_equal))

            def best(k):
                last_step()
                counted(nc.vector.reduce_max(top[k], wide(e_lg), AX))

            def route(n, k):
                if (n, k) == (0, 0):
                    dve.wait_ge(xn_done, TP * PAIRS)
                    dve.wait_ge(xt_ps, PAIRS)
                    dve.wait_ge(s_dump0, 16)
                    for i in range(2):
                        dve.wait_ge(xd_copied[i], 16 * PAIRS // 2)
                    dve.wait_ge(lg_kept, 2 * PAIRS)
                    counted(nc.vector.reduce_max(total, lg[:], AX))
                    last_step()
                    counted(nc.vector.tensor_tensor(wide(e_lg), lg[:], each(total), ALU.subtract))
                if (n, k) == (0, 2):
                    dve.wait_ge(r_exp, 1)
                    counted(nc.vector.reduce_sum(total, wide(e_lg), AX))
                    last_step()
                    counted(nc.vector.reciprocal(total, total))
                if (n, k) == (0, 3):
                    last_step()
                    counted(nc.vector.tensor_tensor(wide(e_lg), wide(e_lg), each(total), ALU.mult))
                if (n, k) == (0, 4):
                    best(0)
                if (n, k) == (0, 5):
                    mark(0)
                if (n, k) == (0, 6):
                    order(0)
                if (n, k) == (0, 7):
                    first_marked(0)
                if (n, k) == (1, 0):
                    one_hot(0)
                if (n, k) == (1, 1):
                    last_step()
                    nc.vector.tensor_copy(hot16[0], hot32[0]).then_inc(r_hot, 1)
                    counted(nc.vector.scalar_tensor_tensor(out=e_lg, in0=hot32[0], scalar=-2.0, in1=e_lg, op0=ALU.mult, op1=ALU.add))
                if (n, k) == (1, 2):
                    best(1)
                if (n, k) == (1, 3):
                    mark(1)
                if (n, k) == (1, 4):
                    order(1)
                if (n, k) == (1, 5):
                    first_marked(1)
                if (n, k) == (1, 6):
                    one_hot(1)
                if (n, k) == (1, 7):
                    last_step()
                    nc.vector.tensor_copy(hot16[1], hot32[1]).then_inc(r_hot, 1)
                    nc.vector.tensor_scalar(xd[:, :, D + 1], rank[0], -1.0, float(NE), ALU.mult, ALU.add).then_inc(r_beside, 1)
                    nc.vector.tensor_copy(xd[:, :, D], const("tok")).then_inc(r_beside, 1)
                    nc.vector.tensor_copy(xd[:, :, D + 2], top[0]).then_inc(r_beside, 1)
                    nc.vector.tensor_copy(xd[:, :, D + 3], top[1]).then_inc(r_beside, 1)

            def attend(n, u, h):
                w = 1 - u
                main, ahead, behind = within(n, 0, PAIRS), within(n, -1, PAIRS - 1), within(n, 1, PAIRS + 1)
                for k in range(2 * G):
                    if isinstance(n, int):
                        route(n, k)
                    if ahead and k < 4:
                        spread_q(n + 1, w, 1, k, None)
                    if k >= 4 and within(n, -1, PAIRS - 2):
                        spread_q(n + 2, u, 0, k - 4, h + 1)
                    if ahead:
                        for t in (2 * k, 2 * k + 1):
                            b_, i, view = task_view(t)
                            dve.wait_ge(mx_ps, 16 * (n + 1) + t + 1)
                            if t % NCH == 0:
                                need(dve, m16_done, 2 * n + b_ + 1)
                            nc.vector.reduce_max(mx[:, b_, :, i], view[:, :, 0:CH * (i + 1)], AX).then_inc(mx_done, 1)
                        if k % 4 == 3:
                            dve.wait_ge(mx_done, 16 * (n + 1) + 8 * (b_ + 1))
                            need(dve, mt_done, 2 * n + b_ + 1)
                            nc.vector.tensor_scalar(mx16[:, b_, :], mx[:, b_].rearrange("p g i -> p (g i)"), -1.0 / MSCALE, None,
                                                    ALU.mult).then_inc(m16_done, 1)
                            dve.wait_ge(m16_done, 2 * (n + 1) + b_ + 1)
                            need(dve, m_out[b_], 16 * (n + 1))
                            nc.vector.transpose(mxt[:, b_, :], mx16[:, b_, :]).then_inc(mt_done, 1)
                    if (k == 1 and behind) or (k == 5 and main):
                        done = 2 * n - 1 if k < 4 else 2 * n
                        dve.wait_ge(ytr_ps, done + 1)
                        need(dve, yt_ps, done)
                        v4 = bank(7).rearrange("p (j s c) -> p j s c", j=2, s=2)
                        for j in range(2):
                            va = v4[:, j, 0, :].rearrange("p (h c) -> p h c", h=HG)[:, :, 0:27].rearrange("p h (g e) -> p h g e", e=9)
                            vb = v4[:, j, 1, :].rearrange("p (h c) -> p h c", h=HG)
                            nc.vector.reciprocal(y_r[:, j, 0, :, :], va[:, :, :, DH]).then_inc(yr_done, 1)
                            nc.vector.reciprocal(y_r[:, j, 1, :, 0], vb[:, :, DH]).then_inc(yr_done, 1)
                        for j in range(2):
                            va = v4[:, j, 0, :].rearrange("p (h c) -> p h c", h=HG)[:, :, 0:27].rearrange("p h (g e) -> p h g e", e=9)
                            vb = v4[:, j, 1, :].rearrange("p (h c) -> p h c", h=HG)
                            yv = y_n[:, j, :].rearrange("p (g h d) -> p h g d", g=G, h=HG)
                            dve.wait_ge(yr_done, 4 * done + 2 * j + 2)
                            nc.vector.tensor_tensor(yv[:, :, 0:3, :], va[:, :, :, 0:DH], y_r[:, j, 0, :, :, None].to_broadcast([P, HG, 3, DH]),
                                                    ALU.mult).then_inc(yn_done, 1)
                            nc.vector.tensor_tensor(yv[:, :, 3, :], vb[:, :, 0:DH], y_r[:, j, 1, :, 0:1].to_broadcast([P, HG, DH]),
                                                    ALU.mult).then_inc(yn_done, 1)
                    if (k == 3 and behind) or (k == 7 and main):
                        done = 2 * n - 1 if k < 4 else 2 * n
                        b_ = 1 if k < 4 else 0
                        dve.wait_ge(out_ps, done + 1)
                        dve.wait_ge(xres_done, n if k < 4 else n + 1)
                        v = w if k < 4 else u
                        rows = x_res[v][:, 2 * b_:2 * b_ + 2, :]
                        nc.vector.tensor_tensor(rows, bank(7)[:, 0:T].rearrange("p (j d) -> p j d", j=2),
                                                rows, ALU.add).then_inc(res_done, 1)

            sweep(dve, attend, -1, 3, 13, 17)

            for e in range(NE):
                u = e % 2
                dve.wait_ge(sl_in[u], 16 * (e // 2 + 1))
                need(dve, moe_out[u], 64 * (e // 2))
                first = meta[u][:, :, 0]
                gate = meta[u][:, :, 1]
                nc.vector.tensor_scalar(first, sl[u][:, :, D + 1], float(e), None, ALU.is_equal).then_inc(d_meta, 1)
                nc.vector.tensor_tensor(meta[u][:, :, 2], sl[u][:, :, D + 2], sl[u][:, :, D + 3], ALU.subtract).then_inc(d_meta, 1)
                nc.vector.tensor_tensor(meta_i[u][:], sl[u][:, :, D], const("dump"), ALU.min).then_inc(idx_done, 1)
                dve.wait_ge(d_meta, 4 * e + 2)
                nc.vector.tensor_tensor(gate, first, meta[u][:, :, 2], ALU.mult).then_inc(d_meta, 1)
                dve.wait_ge(d_meta, 4 * e + 3)
                nc.vector.tensor_tensor(gate, gate, sl[u][:, :, D + 3], ALU.add).then_inc(d_meta, 1)
                dve.wait_ge(d_meta, 4 * e + 4)
                dve.wait_ge(eo_ps, e + 1)
                nc.vector.tensor_tensor(eo[u][:], bank(4 + u).rearrange("p (t d) -> p t d", t=SPE),
                                        gate[:, :, None].to_broadcast([P, SPE, D]), ALU.mult).then_inc(eo_done, 1)

        @block.gpsimd
        def _(pool):
            nc.gpsimd.memset(slot_fill[:, 0:D], 0.0).then_inc(s_fill, 1)
            nc.gpsimd.memset(slot_fill[:, D:ROW], 2.0 * NTOK).then_inc(s_fill, 1)
            for i in range(2):
                nc.gpsimd.memset(vp[i][:], 0.0).then_inc(s_vzero, 1)
            pool.wait_ge(s_vzero, 2)
            for i in range(2):
                for g in range(G):
                    off = (9 * g if g < 3 else 0) + DH
                    ins = nc.gpsimd.memset(vp[i][:, :, G * g:G * g + HG, off:off + 1], 1.0)
            ins.then_inc(s_vones, 1)
            for i in range(2):
                for hh in range(HG):
                    nc.gpsimd.memset(kp[i][hh][:].bitcast(F32), 0.0).then_inc(kp_zero, 1)

            def norm(n, u, h):
                for s in range(2):
                    pool.wait_ge(rot_done, 4 * (n - 2) + 2 * s + 2)
                    nc.gpsimd.tensor_tensor(rot[u][:, 2 * s, :], rot[u][:, 2 * s, :], rot[u][:, 2 * s + 1, :], ALU.add).then_inc(sum_done, 1)
                for s in range(2):
                    pool.wait_ge(high_done, 2 * (n - 2) + s + 1)
                    nc.gpsimd.tensor_tensor(parts[u][:, 2 * s + 1, :], rot[u][:, 2 * s, :], parts[u][:, 2 * s, :], ALU.subtract).then_inc(low_done, 1)

            sweep(pool, norm, 2, 2, 16, 18)

            def add_bias(n, u, h):
                pool.wait_ge(xres_in[u], 16 * (h + 1))
                nc.gpsimd.tensor_tensor(x_res[u], x_res[u], b_all[:, None, :].to_broadcast([P, TP, D]), ALU.add).then_inc(xres_done, 1)

            pool.wait_ge(ball_done, 1)
            for n in range(3):
                add_bias(n, n % 2, n // 2)

            steps = [0]

            def after(ins):
                steps[0] += 1
                ins.then_inc(r_pool, 1)
                pool.wait_ge(r_pool, steps[0])

            pool.wait_ge(r_kept, 4)
            pool.wait_ge(proj_ps, 4 * PAIRS)
            pool.wait_ge(r_beside, 4)
            npt = TILES // NGRP
            tv = [t.rearrange("p (g i e) -> p g i e", g=NGRP, i=npt) for t in tile_total]
            cv = [c.rearrange("p (g i e) -> p g i e", g=NGRP, i=npt) for c in queued]
            after(nc.gpsimd.memset(cv[0][:, :, 0, :], 0.0))
            for k in range(2):
                if k == 1:
                    after(nc.gpsimd.tensor_tensor(cv[1][:, :, 0, :], cv[0][:, :, npt - 1, :], tv[0][:, :, npt - 1, :], ALU.add))
                for i in range(1, npt):
                    after(nc.gpsimd.tensor_tensor(cv[k][:, :, i, :], cv[k][:, :, i - 1, :], tv[k][:, :, i - 1, :], ALU.add))
            xd_i = xd[:].bitcast(I32)
            for k in range(2):
                after(nc.gpsimd.tensor_scalar(place, rank[k], -float(NGRP * CAP), float(NE * NGRP * CAP), ALU.mult, ALU.add))
                after(nc.gpsimd.tensor_tensor(place, place, const("grp"), ALU.add))
                after(nc.gpsimd.tensor_tensor(tmp, ahead_in_tile[k], queued[k], ALU.add))
                after(nc.gpsimd.tensor_tensor(tmp, tmp, hot32[k], ALU.mult))
                halves = wide(tmp)
                for width in (NE // 2, NE // 4, NE // 8):
                    after(nc.gpsimd.tensor_tensor(halves[:, :, 0:width], halves[:, :, 0:width], halves[:, :, width:2 * width], ALU.add))
                after(nc.gpsimd.tensor_scalar(over, halves[:, :, 0], float(CAP), NOWHERE, ALU.is_ge, ALU.mult))
                after(nc.gpsimd.tensor_tensor(pos, halves[:, :, 0], over, ALU.add))
                after(nc.gpsimd.tensor_tensor(pos, pos, place, ALU.add))
                ins = nc.gpsimd.tensor_copy(xd_i[:, :, ROW + k], pos)
                if k == 0:
                    after(ins)
            ins.then_inc(routed, 1)

            pool.wait_ge(s_slot0, 16 * PAIRS)

            def attend(n, u, h):
                add_bias(n, u, h)
                for pair, v, hp in sent_beside(n, u, h):
                    hold(pool, stage_in[v], 16 * (hp + 1), seen_pool)
                    for t in range(TP):
                        for c in range(2):
                            nc.gpsimd.indirect_dma_start(
                                slot_dram, bass.IndirectOffsetOnAxis(ap=stage[v][:].bitcast(I32)[:, t, ROW + c:ROW + c + 1], axis=0),
                                stage[v][:, t, 0:ROW], None, bounds_check=SLOTS - 1, oob_is_err=False).then_inc(scattered[v], 16)

            sweep(pool, attend, 3, 3, 13, 16)

            pool.wait_ge(s_dump0, 16)
            for u in range(2):
                pool.wait_ge(sum_stored[u], 16 * PAIRS // 2)
            for e in range(NE):
                u = e % 2
                pool.wait_ge(idx_done, e + 1)
                pool.wait_ge(eo_done, e + 1)
                if e:
                    pool.wait_ge(moe_out[1 - u], 64 * ((e + 1) // 2))
                for t in range(SPE):
                    nc.gpsimd.indirect_dma_start(
                        acc_dram, bass.IndirectOffsetOnAxis(ap=meta_i[u][:, t:t + 1], axis=0),
                        eo[u][:, t, :], None, bounds_check=NTOK + DUMP - 1, oob_is_err=True,
                        compute_op=ALU.add).then_inc(moe_out[u], 16)


def kernel(**inputs):
    import concourse.bacc as bacc
    from concourse.bass_utils import run_bass_kernel_spmd as run

    x = np.ascontiguousarray(inputs["L0_attn_x"]).reshape(NTOK, D)
    wqkv = np.asarray(inputs["L0_attn_Wqkv"]).reshape(H, 3, DH, D)
    bqkv = np.asarray(inputs["L0_attn_bqkv"]).reshape(H, 3, DH)
    swap = np.arange(P) ^ 1
    wq, wk, wv = (wqkv[:, k].reshape(P, D) for k in range(3))
    bq, bk, bv = (bqkv[:, k].reshape(P) for k in range(3))
    consts, at = constants()
    arrays = {
        "x": x,
        "w_qk": np.ascontiguousarray(np.stack([wq.T, wq[swap].T, wk.T, wk[swap].T], axis=1)),
        "w_vr": np.ascontiguousarray(np.concatenate([wv.T, np.asarray(inputs["L0_ffn_w_router"])], axis=1)),
        "b_qk": np.ascontiguousarray(np.stack([bq, bq[swap], bk, bk[swap]], axis=1)),
        "b_v": np.ascontiguousarray(bv.reshape(P, 1)),
        "w_o": np.ascontiguousarray(np.asarray(inputs["L0_attn_Wproj"]).T),
        "b_o": np.ascontiguousarray(np.broadcast_to(np.asarray(inputs["L0_attn_bproj"]), (P, D))),
        "wi": np.ascontiguousarray(inputs["L0_ffn_wi"]),
        "wo": np.ascontiguousarray(inputs["L0_ffn_wo"]),
        **consts,
    }
    nc = bacc.Bacc("TRN2", target_bir_lowering=False, num_devices=1)
    args = {n: nc.dram_tensor(n, v.shape, mybir.dt.from_np(v.dtype), kind="ExternalInput").ap() for n, v in arrays.items()}
    args["out"] = nc.dram_tensor("out", (NTOK, D), F32, kind="ExternalOutput").ap()
    attend_and_mix(nc, args, at)
    r = run(nc, [arrays], core_ids=[0])
    return r.results[0]["out"].reshape(B, T, D)
```

```python
from contextlib import ExitStack

import numpy as np

import concourse.bass as bass
from concourse import mybir

F32 = mybir.dt.float32
F16 = mybir.dt.float16
I32 = mybir.dt.int32
ALU = mybir.AluOpType
ACT = mybir.ActivationFunctionType
AX = mybir.AxisListType.X

P = 128
B, T, D, H = 32, 256, 128, 16
DH = D // H
NTOK = B * T
TILES = NTOK // P
PAIRS = B // 2
PT = 2 * T
TP = PT // P
G = 4
HG = H // G
TERMS = 3
KR_ROWS = TERMS * HG * DH
M_ROWS = KR_ROWS + HG
CH = 32
NCH = T // CH
NE, CAP, FF = 8, 64, 512
NGRP = 8
SLOTS = NE * NGRP * CAP
ROW = D + 4
XROW = ROW + 2
COPIES = 4
EPS = 1e-5
SCALE = float(DH) ** -0.5
MSCALE = 256.0
BIG = 32768.0
PARTS = 2
SPU = SLOTS // NE // PARTS // P
UNITS = NE * PARTS
DUMP = SPU * P
NOWHERE = 1.0e6


def constants():
    pos = np.arange(T, dtype=np.float32)
    ang = pos[:, None] / (np.float32(10000.0) ** (np.arange(0, DH, 2, dtype=np.float32) / np.float32(DH)))
    rope = np.stack([np.cos(ang), np.sin(ang)], axis=-1).reshape(T, DH).astype(np.float32)
    rt = np.tile(rope.T, (H, 1))
    sign = np.where(np.arange(P) % 2 == 0, -1.0, 1.0).astype(np.float32)[:, None]
    rows = np.arange(P)
    f = {}
    f["rope"] = rt
    f["rope1"] = (np.float32(1.0) - rt) * sign
    f["ident"] = np.eye(P, dtype=np.float32)
    f["order"] = np.tile(8.0 - np.arange(NE), (P, TILES))
    f["grp"] = np.tile(np.arange(TILES) // (TILES // NGRP) * CAP, (P, 1))
    f["tok"] = rows[:, None] + P * np.arange(TILES)[None, :]
    f["dump"] = NTOK + rows[:, None] + P * np.arange(DUMP // P)[None, :]
    f["expert"] = np.tile(np.arange(NE * SPU) // SPU, (P, 1))
    f["head_rows"] = np.stack([(rows < KR_ROWS) & (rows // DH % HG == hh) for hh in range(HG)], 1)
    f["eps"] = np.full((P, 1), EPS)
    at, parts = {}, []
    n = 0
    for name, a in f.items():
        at[name] = (n, n + a.shape[1])
        n += a.shape[1]
        parts.append(a.astype(np.float32))
    packed = np.concatenate(parts, axis=1)

    before = (rows[:, None] < rows[None, :]).astype(np.float16)
    q, r = np.arange(CH), np.arange(CH)
    kmask = np.where(q[None, :] > r[:, None], -BIG, 0.0)
    return {
        "cf": packed,
        "before": before,
        "cmask": np.where(rows[:, None] > rows[None, :], -BIG, 0.0).astype(np.float16),
        "big_id": (np.eye(P) * BIG).astype(np.float16),
        "kmask": np.tile(kmask, (1, G * PT // CH)).astype(np.float16),
        "qhot": np.tile(np.eye(CH) * BIG, (1, G * NCH * HG)).astype(np.float16),
        "kones": np.stack([np.where(np.arange(HG)[:, None] == hh, MSCALE, 0.0) * np.ones((1, G * PT)) for hh in range(HG)]).astype(np.float16),
    }, at


def sweep(eng, body, start, loop_from, loop_to, end):
    for n in range(start, loop_from):
        body(n, n % 2, n // 2)
    with eng.Fori(0, (loop_to - loop_from) // 2) as it:
        for k in range(2):
            n0 = loop_from + k
            body(it * 2 + n0, n0 % 2, it + n0 // 2)
    for n in range(loop_to, end):
        body(n, n % 2, n // 2)


def within(n, lo, hi):
    return lo <= n < hi if isinstance(n, int) else True


def need(eng, sem, value):
    if not isinstance(value, int) or value > 0:
        eng.wait_ge(sem, value)


def hold(eng, sem, value, seen):
    if not isinstance(value, int):
        eng.wait_ge(sem, value)
        eng.sem_inc(seen, 1)
    elif value > 0:
        eng.wait_ge(sem, value)


def vector_masks(n, k):
    if isinstance(n, int) and n == PAIRS - 1:
        return True
    return k % 2 == 1 and within(n, 2, PAIRS)


def units(eng, body, first, last):
    for i in range(first, min(last, 2)):
        body(i, i % 2, i // 2, i, 0)
    for part in range(PARTS):
        lo, hi = max(first, 2, NE * part), min(last, NE * part + NE)
        if lo < hi:
            with eng.Fori(0, (hi - lo) // 2) as it:
                for k in range(2):
                    body(it * 2 + lo + k, k, it + lo // 2, it * 2 + (lo + k - NE * part), part)


def sent_beside(n, u, h):
    if not isinstance(n, int):
        return [(n - 3, 1 - u, h - 1 if u else h - 2)]
    pairs = [n - 3] if 3 <= n < 11 else [2 * n - 14, 2 * n - 13] if 11 <= n < 15 else []
    return [(p, p % 2, p // 2) for p in pairs]


def pair_of(view, n):
    return view[n] if isinstance(n, int) else view[bass.ds(n, 1)].rearrange("a p t d -> p (a t) d")


def attend_and_mix(nc, a, at):
    ctx = ExitStack()
    with ctx:
        def sb(name, shape, dt=F32):
            return ctx.enter_context(nc.sbuf_tensor(name, shape, dt))

        def sem(name):
            return ctx.enter_context(nc.semaphore(name))

        def sem2(name):
            return [sem(f"{name}{i}") for i in range(2)]

        qk_dram = nc.dram_tensor("qk_parts", (PAIRS, 4, P, PT), F16, kind="Internal").ap()
        m_dram = nc.dram_tensor("maxima", (2, 2, P, CH), F16, kind="Internal").ap()
        slot_dram = nc.dram_tensor("slot_rows", (SLOTS, ROW), F32, kind="Internal").ap()
        acc_dram = nc.dram_tensor("sum_rows", (NTOK + DUMP, D), F32, kind="Internal").ap()

        cf = sb("cf_sb", [P, a["cf"].shape[1]])
        def const(name):
            return cf[:, at[name][0]:at[name][1]]
        before = sb("before_sb", [P, P], F16)
        ones16 = sb("ones16", [P, P], F16)
        cmask = sb("cmask_sb", [P, P], F16)
        big_id = sb("big_id_sb", [P, P], F16)
        w_qk = sb("w_qk_sb", [P, 4, P])
        w_vr = sb("w_vr_sb", [P, D + NE])
        w_o = sb("w_o_sb", [P, D])
        b_qk = sb("b_qk_sb", [P, 4])
        b_v = sb("b_v_sb", [P, 1])
        bv_wide = sb("bv_wide", [P, P])
        b_o = sb("b_o_sb", [P, D])
        b_all = sb("b_all", [P, D])

        xd = sb("xd", [P, TILES, XROW])
        v_all = sb("v_all", [P, TILES, D])

        x_in = [sb(f"x_in{i}", [P, TP, D]) for i in range(2)]
        xn = [sb(f"xn{i}", [P, TP, D]) for i in range(2)]
        xt = [sb(f"xt{i}", [P, PT]) for i in range(2)]
        stats = sb("stats", [P, TP, 6])
        mv = sb("mv", [P, TP, 2])
        dev = sb("dev", [P, TP])
        rstd = sb("rstd", [P, TP])
        shift = sb("shift", [P, TP])
        shared = sb("shared", [P, 8 * PT])
        rot = [shared[:, 4 * PT * i:4 * PT * (i + 1)].rearrange("p (j t) -> p j t", j=4) for i in range(2)]
        p0 = [shared[:, HG * T * i:HG * T * (i + 1)].rearrange("p (h t) -> p h t", h=HG) for i in range(2)]
        p1 = [shared[:, 4 * PT + PT * i:4 * PT + PT * (i + 1)].rearrange("p (h t) -> p h t", h=HG) for i in range(2)]
        x_res = [shared[:, 6 * PT + PT * i:6 * PT + PT * (i + 1)].rearrange("p (t d) -> p t d", t=TP) for i in range(2)]
        parts = [sb(f"parts{i}", [P, 4, PT], F16) for i in range(2)]

        qb = [sb(f"qb{i}", [P, G, PT], F16) for i in range(2)]
        kr = [sb(f"kr{i}", [P, G, PT], F16) for i in range(2)]
        qm = [sb(f"qm{i}", [P, G, PT], F16) for i in range(2)]
        kp = [[sb(f"kp{i}{hh}", [P, G, PT], F16) for hh in range(HG)] for i in range(2)]
        qbd = [sb(f"qbd{i}", [P, G, NCH, HG, CH], F16) for i in range(2)]
        mx = sb("mx", [P, 2, G, NCH])
        mx16 = sb("mx16", [P, 2, G * NCH], F16)
        mxt = sb("mxt", [P, 2, CH], F16)
        vp = [sb(f"vp{i}", [P, 2, H, CH]) for i in range(2)]
        y_u = sb("y_u", [P, 2, T])
        y_r = sb("y_r", [P, 2, 2, HG, 3])
        y_n = sb("y_n", [P, 2, D])
        y_t = sb("y_t", [P, T])
        stage = [sb(f"stage{i}", [P, TP, XROW]) for i in range(2)]

        lg = sb("lg", [P, TILES, NE])

        PS = ctx.enter_context(nc.psum_tensor("PS", [P, 8 * 512], F32))

        def bank(k, n=1):
            return PS[:, 512 * k:512 * (k + n)]

        s_cf = sem("const_loaded"); s_w = sem("weights_loaded"); s_init = sem("patterns_loaded")
        s_zero = sem("zeroed"); kp_zero = sem("kp_zeroed"); s_vzero = sem("v_zeroed"); s_vones = sem("v_ones")
        s_fill = sem("slot_fill_set"); s_dump0 = sem("dump_rows_zeroed"); s_slot0 = sem("slot_rows_set")
        x_loaded = sem2("x_loaded"); xd_copied = sem2("xd_copied"); parts_stored = sem2("parts_stored")
        stats_done = sem("stats_done"); mv_done = sem("mv_done"); dev_done = sem("dev_done")
        rstd_done = sem("rstd_done"); shift_done = sem("shift_done"); xn_done = sem("xn_done")
        xt_ps = sem("xt_ps"); xt_done = sem("xt_done")
        v_ps = sem("v_ps"); v_kept = sem("v_kept"); lg_kept = sem("lg_kept")
        proj_ps = sem("proj_ps"); rot_done = sem("rot_done"); sum_done = sem("sum_done")
        high_done = sem("high_done"); low_done = sem("low_done")
        bv_done = sem("bv_wide_done"); ball_ps = sem("ball_ps"); ball_done = sem("ball_done")
        r_dve = sem("route_dve"); r_exp = sem("route_exp"); r_hot = sem("route_hot"); r_ps = sem("route_ps")
        r_kept = sem("route_kept"); r_beside = sem("route_beside"); r_pool = sem("route_pool")
        routed = sem("routed")
        seen_sp = sem("seen_sp"); seen_dve = sem("seen_dve"); seen_pool = sem("seen_pool")

        qb_loaded = sem2("qb_loaded"); kr_loaded = sem2("kr_loaded"); qm_loaded = sem2("qm_loaded"); kp_loaded = sem2("kp_loaded")
        m_out = sem2("m_out"); m_in = sem2("m_in"); stage_in = sem2("stage_in"); scattered = sem2("scattered")
        xres_in = sem2("xres_in"); xres_done = sem("xres_done")
        qbd_done = sem("qbd_done"); mx_ps = sem("mx_ps"); mx_done = sem("mx_done"); m16_done = sem("m16_done"); mt_done = sem("mt_done")
        s0_ps = sem("s0_ps"); s1_ps = sem("s1_ps"); s1_masked = sem("s1_masked"); p0_exp = sem("p0_exp"); p1_exp = sem("p1_exp")
        pv_unit = sem("pv_unit")
        vp_done = [sem("vp_done0"), sem("vp_done1")]
        yu_done = sem("yu_done"); ytr_ps = sem("ytr_ps"); yr_done = sem("yr_done"); yn_done = sem("yn_done")
        yt_ps = sem("yt_ps"); yt_done = sem("yt_done"); out_ps = sem("out_ps"); res_done = sem("res_done")

        sl_in = sem2("sl_in"); wi_in = sem2("wi_in"); wo_in = sem2("wo_in"); d_meta = sem("d_meta"); idx_done = sem("idx_done")
        st_ps = sem("st_ps"); st_done = sem("st_done"); h_ps = sem("h_ps"); h_done = sem("h_done")
        eo_ps = sem("eo_ps"); eo_done = sem("eo_done"); moe_out = [sem2(f"moe_out{t}_") for t in range(SPU)]
        sum_stored = sem2("sum_stored"); out_stored = sem("out_stored")

        x_v = a["x"].rearrange("(n t p) d -> n p t d", t=TP, p=P)
        acc_v = acc_dram[0:NTOK].rearrange("(n t p) d -> n p t d", t=TP, p=P)

        sl = [stage[i] for i in range(2)]
        wi = [qb[i][:, 0:2, :].bitcast(F32).rearrange("p g (c t) -> p (g c) t", t=P) for i in range(2)]
        wo = [qb[i][:, 2:4, :].bitcast(F32).rearrange("p g (c t) -> p (g c) t", t=P) for i in range(2)]
        wi_v = a["wi"].rearrange("e p (c f) -> e p c f", f=P)
        wo_v = a["wo"].rearrange("e (c p) d -> e p c d", p=P)
        unit_slots = slot_dram.rearrange("(e f t p) d -> f e p t d", e=NE, f=PARTS, p=P)
        s_t = [xt[i] for i in range(2)]
        h_t = [rot[i] for i in range(2)]
        eo = [xn[i] for i in range(2)]
        meta = [sb(f"meta{i}", [P, SPU, 4]) for i in range(2)]
        meta_i = [sb(f"meta_i{i}", [P, SPU], I32) for i in range(2)]

        zero_tile = sb("zero_tile", [P, PT])
        slot_fill = sb("slot_fill", [P, ROW])

        def wide(t):
            return t.rearrange("p (t e) -> p t e", e=NE)

        def each(t):
            return t[:, :, None].to_broadcast([P, TILES, NE])
        e_lg, tmp = [x_in[k][:].rearrange("p t d -> p (t d)") for k in range(2)]
        hot32 = [xn[k][:].rearrange("p t d -> p (t d)") for k in range(2)]
        hot16 = [lg[:].bitcast(F16).rearrange("p t e -> p (t e)")[:, PT * k:PT * k + PT] for k in range(2)]
        queued = [xt[k][:] for k in range(2)]
        tile_room = [parts[k][:].bitcast(F32).rearrange("p j t -> p (j t)") for k in range(2)]
        ahead_in_tile = [tile_room[k][:, 0:PT] for k in range(2)]
        tile_total = [tile_room[k][:, PT:2 * PT] for k in range(2)]
        total, top0, top1, rank0, rank1, place, pos, over = [zero_tile[:, TILES * k:TILES * k + TILES] for k in range(8)]
        top, rank = [top0, top1], [rank0, rank1]

        block = ctx.enter_context(nc.Block())

        def task_view(t):
            b_, c = divmod(t, NCH)
            i = NCH - 1 - c // 2 if c % 2 == 0 else NCH // 2 - 1 - c // 2
            if i >= NCH // 2:
                return b_, i, bank(3, 2).rearrange("p (g t) -> p g t", g=G)
            return b_, i, bank(5).rearrange("p (g t) -> p g t", g=G)

        @block.sync
        def _(sp):
            sp.dma_start(x_in[0][:], x_v[0]).then_inc(x_loaded[0], 16)
            sp.dma_start(cf[:], a["cf"]).then_inc(s_cf, 16)
            sp.dma_start(w_qk[:], a["w_qk"]).then_inc(s_w, 16)
            sp.dma_start(w_vr[:], a["w_vr"]).then_inc(s_w, 16)
            sp.dma_start(b_qk[:], a["b_qk"]).then_inc(s_w, 16)
            sp.dma_start(b_v[:], a["b_v"]).then_inc(s_w, 16)
            sp.dma_start(w_o[:], a["w_o"]).then_inc(s_w, 16)
            sp.dma_start(b_o[:], a["b_o"]).then_inc(s_w, 16)
            sp.dma_start(before[:], a["before"]).then_inc(s_w, 16)
            sp.dma_start(cmask[:], a["cmask"]).then_inc(s_w, 16)
            sp.dma_start(big_id[:], a["big_id"]).then_inc(s_w, 16)

            sp.dma_start(x_in[1][:], x_v[1]).then_inc(x_loaded[1], 16)
            sp.wait_ge(s_zero, 2)
            sp.wait_ge(s_fill, 2)
            sp.dma_start(acc_dram[NTOK:].rearrange("(t p) d -> p t d", p=P),
                         zero_tile[:, 0:SPU * D].rearrange("p (t d) -> p t d", d=D)).then_inc(s_dump0, 16)
            slot_v = slot_dram.rearrange("(n t p) d -> n p t d", n=PAIRS, p=P)

            def norm(n, u, h):
                if within(n, 1, PAIRS - 1):
                    need(sp, xn_done, n * TP)
                    sp.dma_start(x_in[1 - u][:], pair_of(x_v, n + 1)).then_inc(x_loaded[1 - u], 16)
                if within(n, 0, PAIRS):
                    fill = slot_fill[:, None, :].to_broadcast([P, SLOTS // P // PAIRS, ROW])
                    sp.dma_start(pair_of(slot_v, n), fill).then_inc(s_slot0, 16)
                if within(n, 1, PAIRS + 1):
                    v = 1 - u
                    sp.wait_ge(xn_done, n * TP)
                    sp.dma_start(xd[:, bass.ds(n * TP - TP, TP), 0:D], xn[v][:]).then_inc(xd_copied[v], 16)
                if within(n, 3, PAIRS + 3):
                    v = 1 - u
                    sp.wait_ge(low_done, 2 * (n - 2))
                    sp.dma_start(qk_dram[bass.ds(n - 3, 1)].rearrange("a x p t -> p (a x) t"),
                                 parts[v][:]).then_inc(parts_stored[v], 16)

            for n in range(3):
                norm(n, n % 2, n // 2)
            with sp.Fori(0, 6) as it:
                norm(it * 2 + 3, 1, it + 1)
                norm(it * 2 + 4, 0, it + 2)
            sp.wait_ge(kp_zero, 8)
            for i in range(2):
                sp.dma_start(kr[i][KR_ROWS:P, :, :].rearrange("p g t -> p (g t)"), a["kmask"]).then_inc(s_init, 16)
                sp.dma_start(qbd[i][KR_ROWS:P].rearrange("p g i h q -> p (g i h q)"), a["qhot"]).then_inc(s_init, 16)
                for hh in range(HG):
                    sp.dma_start(kp[i][hh][KR_ROWS:M_ROWS].rearrange("p g t -> p (g t)"), a["kones"][hh]).then_inc(s_init, 16)

            def part_rows(pair, part):
                return qk_dram[pair, part].rearrange("(g r) t -> r g t", g=G) if isinstance(pair, int) else \
                    qk_dram[bass.ds(pair, 1), part].rearrange("a (g r) t -> r (a g) t", g=G)

            Q_HI, Q_LO, K_HI, K_LO = range(4)

            def load_max_operands(n, v):
                for term, part in enumerate((Q_HI, Q_HI, Q_LO)):
                    sp.dma_start(qb[v][32 * term:32 * term + 32], part_rows(n, part)).then_inc(qb_loaded[v], 16)
                for term, part in enumerate((K_HI, K_LO, K_HI)):
                    sp.dma_start(kr[v][32 * term:32 * term + 32], part_rows(n, part)).then_inc(kr_loaded[v], 16)

            def load_main_operands(n, v):
                for term, part in enumerate((Q_HI, Q_HI, Q_LO)):
                    sp.dma_start(qm[v][32 * term:32 * term + 32], part_rows(n, part)).then_inc(qm_loaded[v], 16)
                for term, part in enumerate((K_HI, K_LO, K_HI)):
                    for hh in range(HG):
                        r0 = 32 * term + DH * hh
                        src = part_rows(n, part)[DH * hh:DH * hh + DH]
                        sp.dma_start(kp[v][hh][r0:r0 + DH], src).then_inc(kp_loaded[v], 16)

            sp.wait_ge(s_init, 16 * 12)
            norm(15, 1, 7)
            sp.wait_ge(parts_stored[0], 16)
            load_max_operands(0, 0)
            norm(16, 0, 8)
            sp.wait_ge(parts_stored[1], 16)
            load_max_operands(1, 1)
            norm(17, 1, 8)
            load_main_operands(0, 0)
            norm(18, 0, 9)
            sp.wait_ge(parts_stored[0], 16 * PAIRS // 2)
            sp.wait_ge(parts_stored[1], 16 * PAIRS // 2)

            def attend(n, u, h):
                w = 1 - u
                if within(n, 0, PAIRS - 2):
                    hold(sp, qbd_done, 8 * (n + 1), seen_sp)
                    hold(sp, mx_ps, 16 * (n + 1), seen_sp)
                    load_max_operands(n + 2, u)
                if within(n, 0, PAIRS):
                    need(sp, sum_stored[u], 16 * h)
                    sp.dma_start(x_res[u], pair_of(x_v, n)).then_inc(xres_in[u], 16)
                for pair, v, hp in sent_beside(n, u, h):
                    if isinstance(n, int) and pair == 0:
                        sp.wait_ge(routed, 1)
                    need(sp, scattered[v], 128 * hp)
                    sp.dma_start(stage[v][:], xd[:, bass.ds(pair * TP, TP), :]).then_inc(stage_in[v], 16)
                if within(n, 0, PAIRS - 1):
                    need(sp, s1_ps, 8 * n)
                    load_main_operands(n + 1, w)
                if within(n, -1, PAIRS - 1):
                    for b_ in range(2):
                        sp.wait_ge(mt_done, 2 * (n + 1) + b_ + 1)
                        sp.dma_start(m_dram[w, b_], mxt[:, b_, :]).then_inc(m_out[b_], 16)
                        sp.wait_ge(m_out[b_], 16 * (n + 2))
                        sp.dma_start(qm[w][KR_ROWS:M_ROWS, :, b_ * T:(b_ + 1) * T],
                                     m_dram[w, b_].rearrange("(r g i) q -> r g (i q)", r=HG, g=G)).then_inc(m_in[b_], 16)
                if within(n, 1, PAIRS + 1):
                    sp.wait_ge(res_done, 2 * n)
                    sp.dma_start(pair_of(acc_v, n - 1), x_res[w]).then_inc(sum_stored[w], 16)

            sweep(sp, attend, -1, 5, 11, 16)

            def load_unit(i, u, h, e, part):
                if isinstance(i, int) and i == 0:
                    for v in range(2):
                        sp.wait_ge(scattered[v], 128 * PAIRS // 2)
                    sp.wait_ge(qbd_done, 8 * PAIRS)
                if within(i, 2, UNITS):
                    hold(sp, st_ps, i - 1, seen_sp)
                    hold(sp, d_meta, 5 * (i - 1), seen_sp)
                sp.dma_start(sl[u][:, 0:SPU, 0:ROW], pair_of(unit_slots[part], e)).then_inc(sl_in[u], 16)
                if within(i, 2, UNITS):
                    hold(sp, h_ps, 2 * (i - 1), seen_sp)
                sp.dma_start(wi[u], pair_of(wi_v, e)).then_inc(wi_in[u], 16)
                if within(i, 1, UNITS):
                    load_second(i - 1, 1 - u, (e - 1) % NE if isinstance(e, int) else e - 1)

            def load_second(i, u, e):
                if within(i, 2, UNITS):
                    hold(sp, eo_ps, i - 1, seen_sp)
                sp.dma_start(wo[u], pair_of(wo_v, e)).then_inc(wo_in[u], 16)

            def copy_rows(part, k):
                if k % (COPIES // SPU) == 0:
                    for v in range(2):
                        sp.wait_ge(moe_out[k // (COPIES // SPU)][v], 16 * (NE // 2) * (part + 1))
                step = NTOK // PARTS // COPIES
                rows = slice(part * NTOK // PARTS + k * step, part * NTOK // PARTS + (k + 1) * step)
                sp.dma_start(a["out"][rows], acc_dram[rows]).then_inc(out_stored, 16)

            units(sp, load_unit, 0, 2)
            attend(PAIRS, 0, PAIRS // 2)
            units(sp, load_unit, 2, NE)
            for i in range(NE, NE + 2):
                load_unit(i, i % 2, i // 2, i - NE, 1)
            units(sp, load_unit, NE + 2, UNITS - COPIES)
            for k in range(COPIES):
                i = UNITS - COPIES + k
                load_unit(i, i % 2, i // 2, i - NE, 1)
                copy_rows(0, k)
            load_second(UNITS - 1, 1, NE - 1)
            for k in range(COPIES):
                copy_rows(1, k)
            sp.wait_ge(out_stored, 16 * COPIES * PARTS)

        @block.tensor
        def _(pe):
            pe.wait_ge(s_cf, 16)
            pe.wait_ge(s_w, 16 * 9)
            ident = const("ident")

            def norm(n, u, h):
                w = 1 - u
                if within(n, 1, PAIRS + 1):
                    pe.wait_ge(xt_done, n)
                    need(pe, v_kept, 2 * (n - 1))
                    need(pe, lg_kept, 2 * (n - 1))
                    for t in range(TP):
                        c = t % 2 * (D + NE)
                        ins = nc.tensor.matmul(bank(4 + t // 2)[:, c:c + D + NE], xt[w][:, P * t:P * t + P], w_vr[:],
                                               start=True, stop=True)
                        if t % 2:
                            ins.then_inc(v_ps, 1)
                    for j in range(2):
                        need(pe, rot_done, 4 * (n - 2) + j + 1)
                        nc.tensor.matmul(bank(j), w_qk[:, j, :], xt[w][:], start=True, stop=True).then_inc(proj_ps, 1)
                if within(n, 0, PAIRS):
                    pe.wait_ge(xn_done, TP * (n + 1))
                    need(pe, xt_done, n - 1)
                    for t in range(TP):
                        ins = nc.tensor.transpose(bank(6 + u)[:, P * t:P * t + P], xn[u][:, t, :], ident)
                    ins.then_inc(xt_ps, 1)
                if within(n, 1, PAIRS + 1):
                    for j in range(2, 4):
                        need(pe, rot_done, 4 * (n - 2) + j + 1)
                        nc.tensor.matmul(bank(j), w_qk[:, j, :], xt[w][:], start=True, stop=True).then_inc(proj_ps, 1)

            sweep(pe, norm, 0, 2, 16, 17)

            pe.wait_ge(s_init, 16 * 12)
            pe.wait_ge(rot_done, 4 * PAIRS)
            pe.wait_ge(v_kept, 2 * PAIRS)
            pe.wait_ge(lg_kept, 2 * PAIRS)
            pe.wait_ge(xt_done, PAIRS)
            pe.wait_ge(bv_done, 1)
            nc.tensor.matmul(bank(7)[:, 0:D], bv_wide[:], w_o[:], start=True, stop=True).then_inc(ball_ps, 1)

            def queues():
                pe.wait_ge(r_hot, 2)
                pe.wait_ge(p0_exp, 16)
                pe.wait_ge(p1_exp, 16)
                pe.wait_ge(res_done, 3)
                for i in range(2):
                    nc.tensor.matmul(bank(i), before[:], hot16[i], start=True, stop=True)
                    nc.tensor.matmul(bank((2, 7)[i]), ones16[:], hot16[i], start=True, stop=True).then_inc(r_ps, 1)
                pe.wait_ge(r_kept, 4)

            def max_task(n, v, t, loads):
                b_, i, view = task_view(t)
                if t % NCH == 0:
                    pe.wait_ge(qbd_done, 8 * n + 4 * (b_ + 1))
                if t == 0:
                    pe.wait_ge(kr_loaded[v], 48 * loads)
                need(pe, mx_done, 16 * n + t - 1)
                for g in range(G):
                    if i:
                        nc.tensor.matmul(view[:, g, 0:CH * i], qbd[b_][0:KR_ROWS, g, i].rearrange("p h q -> p (h q)"),
                                         kr[v][0:KR_ROWS, g, b_ * T:b_ * T + CH * i], start=True, stop=True)
                    ins = nc.tensor.matmul(view[:, g, CH * i:CH * i + CH], qbd[b_][:, g, i].rearrange("p h q -> p (h q)"),
                                           kr[v][:, g, b_ * T + CH * i:b_ * T + CH * i + CH], start=True, stop=True)
                ins.then_inc(mx_ps, 1)

            def slots_transposed(i, u, h):
                pe.wait_ge(sl_in[u], 16 * (h + 1))
                need(pe, st_done, i - 1)
                for t in range(SPU):
                    ins = nc.tensor.transpose(bank(6 + u)[:, P * t:P * t + P], sl[u][:, t, 0:D], ident)
                ins.then_inc(st_ps, 1)

            def first_products(i, u, h):
                pe.wait_ge(st_done, i + 1)
                pe.wait_ge(wi_in[u], 16 * (h + 1))
                need(pe, h_done, 2 * (i - 1))
                for c in range(FF // P):
                    ins = nc.tensor.matmul(bank(2 * u + c // 2)[:, c % 2 * SPU * P:(c % 2 + 1) * SPU * P], wi[u][:, c, :],
                                           s_t[u][:, 0:SPU * P], start=True, stop=True)
                    if c % 2:
                        ins.then_inc(h_ps, 1)

            def attend(n, u, h):
                w = 1 - u
                loads = h + 1 if u == 0 else h + 2
                main, ahead, behind = within(n, 0, PAIRS), within(n, -1, PAIRS - 1), within(n, 1, PAIRS + 1)
                for k in range(2 * G):
                    b_, g = divmod(k, G)
                    if isinstance(n, int) and (n, k) == (2, 0):
                        queues()
                    if main:
                        if k == 0:
                            pe.wait_ge(qm_loaded[u], 48 * (h + 1))
                            pe.wait_ge(kp_loaded[u], 192 * (h + 1))
                        if g == 0:
                            pe.wait_ge(m_in[b_], 16 * (n + 1))
                        need(pe, p0_exp, 8 * n + k)
                        for c in range(2):
                            s0 = bank(c).rearrange("p (h t) -> p h t", h=2)[:, :, 0:P]
                            nc.tensor.matmul(s0, big_id[:], cmask[:, None, :].to_broadcast([P, 2, P]),
                                             start=True, stop=False, skip_group_check=True)
                        for hh in range(HG):
                            ins = nc.tensor.matmul(bank(0, 2)[:, T * hh:T * hh + T],
                                                   kp[u][hh][0:M_ROWS, g, b_ * T:b_ * T + P],
                                                   qm[u][0:M_ROWS, g, b_ * T:b_ * T + T], start=False, stop=True, skip_group_check=True)
                        ins.then_inc(s0_ps, 1)
                    if ahead:
                        max_task(n + 1, w, 2 * k, loads)
                    if main:
                        need(pe, p1_exp, 8 * n + k)
                        if not vector_masks(n, k):
                            nc.tensor.matmul(bank(2), big_id[:], cmask[:, None, :].to_broadcast([P, HG, P]),
                                             start=True, stop=False, skip_group_check=True)
                        for hh in range(HG):
                            ins = nc.tensor.matmul(bank(2)[:, P * hh:P * hh + P],
                                                   kp[u][hh][0:M_ROWS, g, b_ * T + P:b_ * T + T],
                                                   qm[u][0:M_ROWS, g, b_ * T + P:b_ * T + T], start=vector_masks(n, k), stop=True, skip_group_check=True)
                        ins.then_inc(s1_ps, 1)
                    if ahead:
                        max_task(n + 1, w, 2 * k + 1, loads)
                    if isinstance(n, int) and (n, k) == (PAIRS, 2):
                        pe.wait_ge(yu_done, 2 * PAIRS)
                        slots_transposed(0, 0, 0)
                    if isinstance(n, int) and (n, k) == (PAIRS, 3):
                        pe.wait_ge(p0_exp, 8 * PAIRS)
                        first_products(0, 0, 0)
                    if (k in (1, 2, 3) and behind) or (k in (5, 6, 7) and main):
                        done = 2 * n - 1 if k < 4 else 2 * n
                        if k % 4 == 1:
                            pe.wait_ge(yu_done, done + 1)
                            need(pe, res_done, done)
                            for s in range(2):
                                for j in range(2):
                                    ins = nc.tensor.transpose(bank(7)[:, P * (2 * j + s):P * (2 * j + s) + P],
                                                              y_u[:, s, P * j:P * j + P], ident)
                            ins.then_inc(ytr_ps, 1)
                        elif k % 4 == 2:
                            pe.wait_ge(yn_done, 4 * (done + 1))
                            for j in range(2):
                                ins = nc.tensor.transpose(bank(7)[:, P * j:P * j + P], y_n[:, j, :], ident)
                            ins.then_inc(yt_ps, 1)
                        else:
                            pe.wait_ge(yt_done, done + 1)
                            for j in range(2):
                                ins = nc.tensor.matmul(bank(7)[:, P * j:P * j + P], y_t[:, P * j:P * j + P], w_o[:],
                                                       start=True, stop=True)
                            ins.then_inc(out_ps, 1)
                    if (k == 0 and behind) or (k > 0 and main):
                        m = 8 * n + k - 1
                        pb, pg = divmod((k - 1) % 8, G)
                        q = (k - 1) % 2
                        pe.wait_ge(p0_exp, m + 1)
                        pe.wait_ge(p1_exp, m + 1)
                        if pg == 0:
                            pe.wait_ge(vp_done[pb], 4 * (n + 1))
                            need(pe, yu_done, 2 * n + pb)
                        s = 0 if pg < 3 else 1
                        for j in range(2):
                            for hh in range(HG):
                                dst = bank(6)[32 * hh:32 * hh + 32, s * T + P * j:(s + 1) * T]
                                src = (p0[q], p1[q])[j][:, hh, :]
                                ins = nc.tensor.matmul(dst, vp[pb][:, j, G * pg + hh, :], src, start=(pg == 0 and j == 0),
                                                       stop=(pg >= 2 and j == 1), skip_group_check=True)
                        ins.then_inc(pv_unit, 1)

            sweep(pe, attend, -1, 3, 13, 17)

            def unit(i, u, h, e, part):
                v = 1 - u
                if within(i, 1, UNITS):
                    first_products(i, u, h)
                if isinstance(i, int) and i == 0:
                    pe.wait_ge(res_done, 2 * PAIRS)
                if within(i, 0, UNITS - 1):
                    slots_transposed(i + 1, v, h if u == 0 else h + 1)
                if within(i, 1, UNITS + 1):
                    pe.wait_ge(h_done, 2 * i)
                    pe.wait_ge(wo_in[v], 16 * (h if u == 0 else h + 1))
                    need(pe, eo_done, i - 2)
                    for t in range(SPU):
                        for c in range(FF // P):
                            ins = nc.tensor.matmul(bank(4 + v)[:, P * t:P * t + P], h_t[v][:, c, P * t:P * t + P], wo[v][:, c, :],
                                                   start=(c == 0), stop=(c == FF // P - 1))
                    ins.then_inc(eo_ps, 1)

            units(pe, unit, 0, UNITS - 2)
            for i in range(UNITS - 2, UNITS + 1):
                unit(i, i % 2, i // 2, None, None)

        @block.scalar
        def _(act):
            def norm(n, u, h):
                if within(n, 0, PAIRS):
                    act.wait_ge(mv_done, TP * (n + 1))
                    need(act, rstd_done, n)
                    if isinstance(n, int) and n == 0:
                        act.wait_ge(s_cf, 16)
                    nc.scalar.activation(dev[:], mv[:, :, 1], ACT.Sqrt, bias=const("eps")).then_inc(dev_done, 1)
                if within(n, 1, PAIRS + 1):
                    for s in range(2):
                        act.wait_ge(v_ps, 2 * (n - 1) + s + 1)
                        src = bank(4 + s)[:, 0:2 * (D + NE)].rearrange("p (t c) -> p t c", t=2)[:, :, 0:D]
                        nc.scalar.copy(v_all[:, bass.ds(n * TP - TP + 2 * s, 2), :], src).then_inc(v_kept, 1)
                if within(n, 0, PAIRS):
                    act.wait_ge(shift_done, n + 1)
                    if within(n, 2, 99):
                        need(act, xt_ps, n - 1)
                        act.wait_ge(xd_copied[u], 16 * h)
                    for t in range(TP):
                        nc.scalar.activation(xn[u][:, t, :], x_in[u][:, t, :], ACT.Identity, bias=shift[:, t:t + 1],
                                             scale=rstd[:, t:t + 1]).then_inc(xn_done, 1)
                    act.wait_ge(xt_ps, n + 1)
                    need(act, v_ps, 2 * (n - 1))
                    need(act, proj_ps, 4 * (n - 1))
                    nc.scalar.copy(xt[u][:], bank(6 + u)).then_inc(xt_done, 1)
                if within(n, 2, PAIRS + 2):
                    for s in range(2):
                        act.wait_ge(sum_done, 2 * (n - 2) + s + 1)
                        if within(n, 4, PAIRS + 2):
                            need(act, parts_stored[u], 16 * (h - 1))
                        nc.scalar.copy(parts[u][:, 2 * s, :], rot[u][:, 2 * s, :]).then_inc(high_done, 1)

            for n in range(4):
                norm(n, n % 2, n // 2)
            with act.Fori(0, 6) as it:
                norm(it * 2 + 4, 0, it + 2)
                norm(it * 2 + 5, 1, it + 2)
            for n in range(16, 18):
                norm(n, n % 2, n // 2)

            act.wait_ge(low_done, 2 * PAIRS)

            def spread_v(n, b_, j):
                src = v_all[:, bass.ds(n * TP + 2 * b_ + j, 1), :].rearrange("p a (g h d) -> p (a g) h d", g=G, h=HG)
                for g in range(G):
                    off = 9 * g if g < 3 else 0
                    ins = nc.scalar.copy(vp[b_][:, j, G * g:G * g + HG, off:off + DH], src[:, g])
                    if g % 2:
                        ins.then_inc(vp_done[b_], 1)

            def attend(n, u, h):
                main, behind = within(n, 0, PAIRS), within(n, 1, PAIRS + 1)
                if isinstance(n, int) and n == -1:
                    act.wait_ge(s_vones, 1)
                    spread_v(0, 0, 0)
                    spread_v(0, 0, 1)
                for k in range(2 * G):
                    q = k % 2
                    if isinstance(n, int) and (n, k) == (0, 1):
                        act.wait_ge(r_dve, 2)
                        nc.scalar.activation(e_lg, e_lg, ACT.Exp).then_inc(r_exp, 1)
                    if isinstance(n, int) and (n, k) == (2, 0):
                        for i in range(2):
                            act.wait_ge(parts_stored[i], 16 * PAIRS // 2)
                        act.wait_ge(r_ps, 2)
                        for i in range(2):
                            nc.scalar.copy(ahead_in_tile[i], bank(i)).then_inc(r_kept, 1)
                            nc.scalar.copy(tile_total[i], bank((2, 7)[i])).then_inc(r_kept, 1)
                    if main:
                        m = 8 * n + k
                        act.wait_ge(s0_ps, m + 1)
                        need(act, pv_unit, m - 1)
                        nc.scalar.activation(p0[q].rearrange("p h t -> p (h t)"), bank(0, 2), ACT.Exp, scale=SCALE).then_inc(p0_exp, 1)
                        if vector_masks(n, k):
                            masked_here = k if isinstance(n, int) and n == PAIRS - 1 else k // 2
                            act.wait_ge(s1_masked, 4 * (n - 2) + masked_here + 1)
                        else:
                            act.wait_ge(s1_ps, m + 1)
                        nc.scalar.activation(p1[q].rearrange("p h t -> p (h t)"), bank(2), ACT.Exp, scale=SCALE).then_inc(p1_exp, 1)
                    if (k == 0 and behind) or (k == 4 and main):
                        done = 2 * n - 1 if k < 4 else 2 * n
                        act.wait_ge(pv_unit, 8 * n if k == 0 else 8 * n + 4)
                        need(act, ytr_ps, done)
                        nc.scalar.copy(y_u[:].rearrange("p s t -> p (s t)"), bank(6)).then_inc(yu_done, 1)
                    if k in (1, 2) and main:
                        if k == 1:
                            need(act, pv_unit, 8 * n)
                        spread_v(n, 1, k - 1)
                    if k in (5, 6) and within(n, 0, PAIRS - 1):
                        if k == 5:
                            act.wait_ge(pv_unit, 8 * n + 4)
                        spread_v(n + 1, 0, k - 5)
                    if (k == 2 and behind) or (k == 6 and main):
                        done = 2 * n - 1 if k < 4 else 2 * n
                        act.wait_ge(yt_ps, done + 1)
                        need(act, out_ps, done)
                        nc.scalar.copy(y_t[:], bank(7)[:, 0:T]).then_inc(yt_done, 1)

            sweep(act, attend, -1, 3, 13, 17)

            def slots_kept(i, u):
                act.wait_ge(st_ps, i + 1)
                need(act, h_ps, 2 * (i - 1))
                nc.scalar.copy(s_t[u][:, 0:SPU * P], bank(6 + u)[:, 0:SPU * P]).then_inc(st_done, 1)

            def unit(i, u, h, e, part):
                if isinstance(i, int) and i == 1:
                    for v in range(2):
                        act.wait_ge(sum_stored[v], 16 * PAIRS // 2)
                for j in range(2):
                    act.wait_ge(h_ps, 2 * i + j + 1)
                    need(act, eo_ps, i - 1)
                    nc.scalar.activation(h_t[u][:, 2 * j:2 * j + 2, 0:SPU * P], bank(2 * u + j).rearrange("p (c t) -> p c t", c=2),
                                         ACT.Gelu_apprx_tanh).then_inc(h_done, 1)
                if within(i, 0, UNITS - 1):
                    slots_kept(i + 1, 1 - u)

            slots_kept(0, 0)
            units(act, unit, 0, UNITS - 2)
            for i in range(UNITS - 2, UNITS):
                unit(i, i % 2, i // 2, None, None)

        @block.vector
        def _(dve):
            nc.vector.memset(zero_tile[:], 0.0).then_inc(s_zero, 1)
            nc.vector.memset(ones16[:], 1.0).then_inc(s_zero, 1)
            dve.wait_ge(s_zero, 2)
            tables = [const("rope"), const("rope1"), const("rope"), const("rope1")]

            def rotate(n, u, j):
                if isinstance(n, int) and (n, j) == (2, 0):
                    dve.wait_ge(s_w, 16 * 9)
                    dve.wait_ge(s_cf, 16)
                dve.wait_ge(proj_ps, 4 * (n - 2) + j + 1)
                if within(n, 4, 99):
                    need(dve, low_done, 2 * (n - 3))
                nc.vector.scalar_tensor_tensor(
                    out=rot[u][:, j, :].rearrange("p (b t) -> p b t", b=2), in0=bank(j).rearrange("p (b t) -> p b t", b=2),
                    scalar=b_qk[:, j:j + 1], in1=tables[j][:, None, :].to_broadcast([P, 2, T]),
                    op0=ALU.add, op1=ALU.mult).then_inc(rot_done, 1)

            def norm(n, u, h):
                if within(n, 2, PAIRS + 2):
                    for s in range(2):
                        dve.wait_ge(v_ps, 2 * (n - 2) + s + 1)
                        dve.wait_ge(v_kept, 2 * (n - 2) + s + 1)
                        src = bank(4 + s)[:, 0:2 * (D + NE)].rearrange("p (t c) -> p t c", t=2)[:, :, D:D + NE]
                        nc.vector.tensor_copy(lg[:, bass.ds(n * TP - 2 * TP + 2 * s, 2), :], src).then_inc(lg_kept, 1)
                if within(n, 0, PAIRS):
                    dve.wait_ge(x_loaded[u], 16 * (h + 1))
                    for t in range(TP):
                        nc.vector.bn_stats(stats[:, t, :], x_in[u][:, t, :]).then_inc(stats_done, 1)
                    for t in range(TP):
                        hold(dve, stats_done, TP * n + t + 1, seen_dve)
                        nc.vector.bn_aggr(mv[:, t, :], stats[:, t, :]).then_inc(mv_done, 1)
                if within(n, 2, PAIRS + 2):
                    rotate(n, u, 0)
                if within(n, 0, PAIRS):
                    dve.wait_ge(dev_done, n + 1)
                    need(dve, xn_done, TP * n)
                    nc.vector.reciprocal(rstd[:], dev[:]).then_inc(rstd_done, 1)
                    dve.wait_ge(rstd_done, n + 1)
                    nc.vector.scalar_tensor_tensor(out=shift[:], in0=mv[:, :, 0], scalar=-1.0, in1=rstd[:],
                                                   op0=ALU.mult, op1=ALU.mult).then_inc(shift_done, 1)
                if within(n, 2, PAIRS + 2):
                    rotate(n, u, 1)
                    rotate(n, u, 2)
                    rotate(n, u, 3)

            for n in range(4):
                norm(n, n % 2, n // 2)
            with dve.Fori(0, 6) as it:
                norm(it * 2 + 4, 0, it + 2)
                norm(it * 2 + 5, 1, it + 2)
            for n in range(16, 18):
                norm(n, n % 2, n // 2)

            nc.vector.tensor_scalar(bv_wide[:], zero_tile[:, 0:P], b_v[:, 0:1], None, ALU.add).then_inc(bv_done, 1)
            dve.wait_ge(ball_ps, 1)
            nc.vector.tensor_tensor(b_all[:], bank(7)[:, 0:D], b_o[:], ALU.add).then_inc(ball_done, 1)

            dve.wait_ge(s_init, 16 * 12)
            masks = const("head_rows")

            def spread_q(n, v, b_, hh, h):
                if hh == 0 and b_ == 0:
                    dve.wait_ge(qb_loaded[v], 48 * (h + 1))
                if hh == 0:
                    need(dve, mx_ps, 16 * (n - 1) + 8 * (b_ + 1))
                nc.vector.tensor_scalar(qbd[b_][0:KR_ROWS, :, :, hh, :],
                                        qb[v][0:KR_ROWS, :, b_ * T:b_ * T + T].rearrange("p g (i q) -> p g i q", q=CH),
                                        masks[0:KR_ROWS, hh:hh + 1], None, ALU.mult).then_inc(qbd_done, 1)

            for hh in range(HG):
                spread_q(0, 0, 0, hh, 0)

            steps = [0]

            def last_step():
                if steps[0]:
                    dve.wait_ge(r_dve, steps[0])

            def counted(ins):
                steps[0] += 1
                ins.then_inc(r_dve, 1)

            def mark(k):
                last_step()
                counted(nc.vector.tensor_tensor(wide(tmp), wide(e_lg), each(top[k]), ALU.is_equal))

            def order(k):
                last_step()
                counted(nc.vector.tensor_tensor(tmp, tmp, const("order"), ALU.mult))

            def first_marked(k):
                last_step()
                counted(nc.vector.reduce_max(rank[k], wide(tmp), AX))

            def one_hot(k):
                last_step()
                counted(nc.vector.tensor_tensor(wide(hot32[k]), wide(tmp), each(rank[k]), ALU.is_equal))

            def best(k):
                last_step()
                counted(nc.vector.reduce_max(top[k], wide(e_lg), AX))

            def route(n, k):
                if (n, k) == (0, 0):
                    dve.wait_ge(xn_done, TP * PAIRS)
                    dve.wait_ge(xt_ps, PAIRS)
                    dve.wait_ge(s_dump0, 16)
                    for i in range(2):
                        dve.wait_ge(xd_copied[i], 16 * PAIRS // 2)
                    dve.wait_ge(lg_kept, 2 * PAIRS)
                    counted(nc.vector.reduce_max(total, lg[:], AX))
                    last_step()
                    counted(nc.vector.tensor_tensor(wide(e_lg), lg[:], each(total), ALU.subtract))
                if (n, k) == (0, 2):
                    dve.wait_ge(r_exp, 1)
                    counted(nc.vector.reduce_sum(total, wide(e_lg), AX))
                    last_step()
                    counted(nc.vector.reciprocal(total, total))
                if (n, k) == (0, 3):
                    last_step()
                    counted(nc.vector.tensor_tensor(wide(e_lg), wide(e_lg), each(total), ALU.mult))
                if (n, k) == (0, 4):
                    best(0)
                if (n, k) == (0, 5):
                    mark(0)
                if (n, k) == (0, 6):
                    order(0)
                if (n, k) == (0, 7):
                    first_marked(0)
                if (n, k) == (1, 0):
                    one_hot(0)
                if (n, k) == (1, 1):
                    last_step()
                    nc.vector.tensor_copy(hot16[0], hot32[0]).then_inc(r_hot, 1)
                    counted(nc.vector.scalar_tensor_tensor(out=e_lg, in0=hot32[0], scalar=-2.0, in1=e_lg, op0=ALU.mult, op1=ALU.add))
                if (n, k) == (1, 2):
                    best(1)
                if (n, k) == (1, 3):
                    mark(1)
                if (n, k) == (1, 4):
                    order(1)
                if (n, k) == (1, 5):
                    first_marked(1)
                if (n, k) == (1, 6):
                    one_hot(1)
                if (n, k) == (1, 7):
                    last_step()
                    nc.vector.tensor_copy(hot16[1], hot32[1]).then_inc(r_hot, 1)
                    nc.vector.tensor_scalar(xd[:, :, D + 1], rank[0], -1.0, float(NE), ALU.mult, ALU.add).then_inc(r_beside, 1)
                    nc.vector.tensor_copy(xd[:, :, D], const("tok")).then_inc(r_beside, 1)
                    nc.vector.tensor_copy(xd[:, :, D + 2], top[0]).then_inc(r_beside, 1)
                    nc.vector.tensor_copy(xd[:, :, D + 3], top[1]).then_inc(r_beside, 1)

            def attend(n, u, h):
                w = 1 - u
                main, ahead, behind = within(n, 0, PAIRS), within(n, -1, PAIRS - 1), within(n, 1, PAIRS + 1)
                for k in range(2 * G):
                    if isinstance(n, int):
                        route(n, k)
                    if ahead and k < 4:
                        spread_q(n + 1, w, 1, k, None)
                    if k >= 4 and within(n, -1, PAIRS - 2):
                        spread_q(n + 2, u, 0, k - 4, h + 1)
                    for t in (2 * k, 2 * k + 1):
                        if t % 2 and vector_masks(n, k):
                            dve.wait_ge(s1_ps, 8 * n + k + 1)
                            s1 = bank(2).rearrange("p (h t) -> p h t", h=HG)
                            nc.vector.scalar_tensor_tensor(out=s1, in0=cmask[:, None, :].to_broadcast([P, HG, P]), scalar=BIG, in1=s1,
                                                           op0=ALU.mult, op1=ALU.add).then_inc(s1_masked, 1)
                        if ahead:
                            b_, i, view = task_view(t)
                            dve.wait_ge(mx_ps, 16 * (n + 1) + t + 1)
                            if t % NCH == 0:
                                need(dve, m16_done, 2 * n + b_ + 1)
                            nc.vector.reduce_max(mx[:, b_, :, i], view[:, :, 0:CH * (i + 1)], AX).then_inc(mx_done, 1)
                    if ahead:
                        if k % 4 == 3:
                            dve.wait_ge(mx_done, 16 * (n + 1) + 8 * (b_ + 1))
                            need(dve, mt_done, 2 * n + b_ + 1)
                            nc.vector.tensor_scalar(mx16[:, b_, :], mx[:, b_].rearrange("p g i -> p (g i)"), -1.0 / MSCALE, None,
                                                    ALU.mult).then_inc(m16_done, 1)
                            dve.wait_ge(m16_done, 2 * (n + 1) + b_ + 1)
                            need(dve, m_out[b_], 16 * (n + 1))
                            nc.vector.transpose(mxt[:, b_, :], mx16[:, b_, :]).then_inc(mt_done, 1)
                    if (k == 1 and behind) or (k == 5 and main):
                        done = 2 * n - 1 if k < 4 else 2 * n
                        dve.wait_ge(ytr_ps, done + 1)
                        need(dve, yt_ps, done)
                        v4 = bank(7).rearrange("p (j s c) -> p j s c", j=2, s=2)
                        for j in range(2):
                            va = v4[:, j, 0, :].rearrange("p (h c) -> p h c", h=HG)[:, :, 0:27].rearrange("p h (g e) -> p h g e", e=9)
                            vb = v4[:, j, 1, :].rearrange("p (h c) -> p h c", h=HG)
                            nc.vector.reciprocal(y_r[:, j, 0, :, :], va[:, :, :, DH]).then_inc(yr_done, 1)
                            nc.vector.reciprocal(y_r[:, j, 1, :, 0], vb[:, :, DH]).then_inc(yr_done, 1)
                        for j in range(2):
                            va = v4[:, j, 0, :].rearrange("p (h c) -> p h c", h=HG)[:, :, 0:27].rearrange("p h (g e) -> p h g e", e=9)
                            vb = v4[:, j, 1, :].rearrange("p (h c) -> p h c", h=HG)
                            yv = y_n[:, j, :].rearrange("p (g h d) -> p h g d", g=G, h=HG)
                            dve.wait_ge(yr_done, 4 * done + 2 * j + 2)
                            nc.vector.tensor_tensor(yv[:, :, 0:3, :], va[:, :, :, 0:DH], y_r[:, j, 0, :, :, None].to_broadcast([P, HG, 3, DH]),
                                                    ALU.mult).then_inc(yn_done, 1)
                            nc.vector.tensor_tensor(yv[:, :, 3, :], vb[:, :, 0:DH], y_r[:, j, 1, :, 0:1].to_broadcast([P, HG, DH]),
                                                    ALU.mult).then_inc(yn_done, 1)
                    if (k == 3 and behind) or (k == 7 and main):
                        done = 2 * n - 1 if k < 4 else 2 * n
                        b_ = 1 if k < 4 else 0
                        dve.wait_ge(out_ps, done + 1)
                        dve.wait_ge(xres_done, n if k < 4 else n + 1)
                        v = w if k < 4 else u
                        rows = x_res[v][:, 2 * b_:2 * b_ + 2, :]
                        nc.vector.tensor_tensor(rows, bank(7)[:, 0:T].rearrange("p (j d) -> p j d", j=2),
                                                rows, ALU.add).then_inc(res_done, 1)

            sweep(dve, attend, -1, 3, 13, 17)

            def gates(i, u, h, e):
                first = meta[u][:, :, 0]
                gate = meta[u][:, :, 1]
                slots = sl[u][:, 0:SPU]
                dve.wait_ge(sl_in[u], 16 * (h + 1))
                need(dve, idx_done, i - 1)
                need(dve, eo_done, i - 1)
                nc.vector.tensor_tensor(first, slots[:, :, D + 1], const("expert")[:, bass.ds(e * SPU, SPU)],
                                        ALU.is_equal).then_inc(d_meta, 1)
                nc.vector.tensor_tensor(meta[u][:, :, 2], slots[:, :, D + 2], slots[:, :, D + 3], ALU.subtract).then_inc(d_meta, 1)
                nc.vector.tensor_tensor(meta[u][:, :, 3], slots[:, :, D], const("dump"), ALU.min).then_inc(d_meta, 1)
                dve.wait_ge(d_meta, 5 * i + 2)
                nc.vector.tensor_tensor(gate, first, meta[u][:, :, 2], ALU.mult).then_inc(d_meta, 1)
                dve.wait_ge(d_meta, 5 * i + 4)
                nc.vector.tensor_tensor(gate, gate, slots[:, :, D + 3], ALU.add).then_inc(d_meta, 1)

            def gated(i, u, h):
                dve.wait_ge(d_meta, 5 * i + 5)
                for t in range(SPU):
                    need(dve, moe_out[t][u], 16 * h)
                nc.vector.tensor_copy(meta_i[u][:], meta[u][:, :, 3]).then_inc(idx_done, 1)
                dve.wait_ge(eo_ps, i + 1)
                nc.vector.tensor_tensor(eo[u][:, 0:SPU, :], bank(4 + u)[:, 0:SPU * D].rearrange("p (t d) -> p t d", t=SPU),
                                        meta[u][:, :, 1][:, :, None].to_broadcast([P, SPU, D]), ALU.mult).then_inc(eo_done, 1)

            def unit(i, u, h, e, part):
                gates(i, u, h, e)
                if within(i, 1, UNITS):
                    gated(i - 1, 1 - u, h if u else h - 1)

            units(dve, unit, 0, UNITS)
            gated(UNITS - 1, 1, UNITS // 2 - 1)

        @block.gpsimd
        def _(pool):
            nc.gpsimd.memset(slot_fill[:, 0:D], 0.0).then_inc(s_fill, 1)
            nc.gpsimd.memset(slot_fill[:, D:ROW], 2.0 * NTOK).then_inc(s_fill, 1)
            for i in range(2):
                nc.gpsimd.memset(vp[i][:], 0.0).then_inc(s_vzero, 1)
            pool.wait_ge(s_vzero, 2)
            for i in range(2):
                for g in range(G):
                    off = (9 * g if g < 3 else 0) + DH
                    ins = nc.gpsimd.memset(vp[i][:, :, G * g:G * g + HG, off:off + 1], 1.0)
            ins.then_inc(s_vones, 1)
            for i in range(2):
                for hh in range(HG):
                    nc.gpsimd.memset(kp[i][hh][:].bitcast(F32), 0.0).then_inc(kp_zero, 1)

            def norm(n, u, h):
                for s in range(2):
                    pool.wait_ge(rot_done, 4 * (n - 2) + 2 * s + 2)
                    nc.gpsimd.tensor_tensor(rot[u][:, 2 * s, :], rot[u][:, 2 * s, :], rot[u][:, 2 * s + 1, :], ALU.add).then_inc(sum_done, 1)
                for s in range(2):
                    pool.wait_ge(high_done, 2 * (n - 2) + s + 1)
                    nc.gpsimd.tensor_tensor(parts[u][:, 2 * s + 1, :], rot[u][:, 2 * s, :], parts[u][:, 2 * s, :], ALU.subtract).then_inc(low_done, 1)

            sweep(pool, norm, 2, 2, 16, 18)

            def add_bias(n, u, h):
                pool.wait_ge(xres_in[u], 16 * (h + 1))
                nc.gpsimd.tensor_tensor(x_res[u], x_res[u], b_all[:, None, :].to_broadcast([P, TP, D]), ALU.add).then_inc(xres_done, 1)

            pool.wait_ge(ball_done, 1)
            for n in range(3):
                add_bias(n, n % 2, n // 2)

            steps = [0]

            def after(ins):
                steps[0] += 1
                ins.then_inc(r_pool, 1)
                pool.wait_ge(r_pool, steps[0])

            pool.wait_ge(r_kept, 4)
            pool.wait_ge(proj_ps, 4 * PAIRS)
            pool.wait_ge(r_beside, 4)
            npt = TILES // NGRP
            tv = [t.rearrange("p (g i e) -> p g i e", g=NGRP, i=npt) for t in tile_total]
            cv = [c.rearrange("p (g i e) -> p g i e", g=NGRP, i=npt) for c in queued]
            after(nc.gpsimd.memset(cv[0][:, :, 0, :], 0.0))
            for k in range(2):
                if k == 1:
                    after(nc.gpsimd.tensor_tensor(cv[1][:, :, 0, :], cv[0][:, :, npt - 1, :], tv[0][:, :, npt - 1, :], ALU.add))
                for i in range(1, npt):
                    after(nc.gpsimd.tensor_tensor(cv[k][:, :, i, :], cv[k][:, :, i - 1, :], tv[k][:, :, i - 1, :], ALU.add))
            xd_i = xd[:].bitcast(I32)
            for k in range(2):
                after(nc.gpsimd.tensor_scalar(place, rank[k], -float(NGRP * CAP), float(NE * NGRP * CAP), ALU.mult, ALU.add))
                after(nc.gpsimd.tensor_tensor(place, place, const("grp"), ALU.add))
                after(nc.gpsimd.tensor_tensor(tmp, ahead_in_tile[k], queued[k], ALU.add))
                after(nc.gpsimd.tensor_tensor(tmp, tmp, hot32[k], ALU.mult))
                halves = wide(tmp)
                for width in (NE // 2, NE // 4, NE // 8):
                    after(nc.gpsimd.tensor_tensor(halves[:, :, 0:width], halves[:, :, 0:width], halves[:, :, width:2 * width], ALU.add))
                after(nc.gpsimd.tensor_scalar(over, halves[:, :, 0], float(CAP), NOWHERE, ALU.is_ge, ALU.mult))
                after(nc.gpsimd.tensor_tensor(pos, halves[:, :, 0], over, ALU.add))
                after(nc.gpsimd.tensor_tensor(pos, pos, place, ALU.add))
                ins = nc.gpsimd.tensor_copy(xd_i[:, :, ROW + k], pos)
                if k == 0:
                    after(ins)
            ins.then_inc(routed, 1)

            pool.wait_ge(s_slot0, 16 * PAIRS)

            def attend(n, u, h):
                add_bias(n, u, h)
                for pair, v, hp in sent_beside(n, u, h):
                    hold(pool, stage_in[v], 16 * (hp + 1), seen_pool)
                    for t in range(TP):
                        for c in range(2):
                            nc.gpsimd.indirect_dma_start(
                                slot_dram, bass.IndirectOffsetOnAxis(ap=stage[v][:].bitcast(I32)[:, t, ROW + c:ROW + c + 1], axis=0),
                                stage[v][:, t, 0:ROW], None, bounds_check=SLOTS - 1, oob_is_err=False).then_inc(scattered[v], 16)

            sweep(pool, attend, 3, 3, 11, 16)

            pool.wait_ge(s_dump0, 16)
            for u in range(2):
                pool.wait_ge(sum_stored[u], 16 * PAIRS // 2)

            def unit(i, u, h, e, part):
                hold(pool, idx_done, i + 1, seen_pool)
                hold(pool, eo_done, i + 1, seen_pool)
                for t in range(SPU):
                    hold(pool, moe_out[t][1 - u], 16 * (h + 1 if u else h), seen_pool)
                    nc.gpsimd.indirect_dma_start(
                        acc_dram, bass.IndirectOffsetOnAxis(ap=meta_i[u][:, t:t + 1], axis=0),
                        eo[u][:, t, :], None, bounds_check=NTOK + DUMP - 1, oob_is_err=True,
                        compute_op=ALU.add).then_inc(moe_out[t][u], 16)

            units(pool, unit, 0, UNITS)


def kernel(**inputs):
    import concourse.bacc as bacc
    from concourse.bass_utils import run_bass_kernel_spmd as run

    x = np.ascontiguousarray(inputs["L0_attn_x"]).reshape(NTOK, D)
    wqkv = np.asarray(inputs["L0_attn_Wqkv"]).reshape(H, 3, DH, D)
    bqkv = np.asarray(inputs["L0_attn_bqkv"]).reshape(H, 3, DH)
    swap = np.arange(P) ^ 1
    wq, wk, wv = (wqkv[:, k].reshape(P, D) for k in range(3))
    bq, bk, bv = (bqkv[:, k].reshape(P) for k in range(3))
    consts, at = constants()
    arrays = {
        "x": x,
        "w_qk": np.ascontiguousarray(np.stack([wq.T, wq[swap].T, wk.T, wk[swap].T], axis=1)),
        "w_vr": np.ascontiguousarray(np.concatenate([wv.T, np.asarray(inputs["L0_ffn_w_router"])], axis=1)),
        "b_qk": np.ascontiguousarray(np.stack([bq, bq[swap], bk, bk[swap]], axis=1)),
        "b_v": np.ascontiguousarray(bv.reshape(P, 1)),
        "w_o": np.ascontiguousarray(np.asarray(inputs["L0_attn_Wproj"]).T),
        "b_o": np.ascontiguousarray(np.broadcast_to(np.asarray(inputs["L0_attn_bproj"]), (P, D))),
        "wi": np.ascontiguousarray(inputs["L0_ffn_wi"]),
        "wo": np.ascontiguousarray(inputs["L0_ffn_wo"]),
        **consts,
    }
    nc = bacc.Bacc("TRN2", target_bir_lowering=False, num_devices=1)
    args = {n: nc.dram_tensor(n, v.shape, mybir.dt.from_np(v.dtype), kind="ExternalInput").ap() for n, v in arrays.items()}
    args["out"] = nc.dram_tensor("out", (NTOK, D), F32, kind="ExternalOutput").ap()
    attend_and_mix(nc, args, at)
    r = run(nc, [arrays], core_ids=[0])
    return r.results[0]["out"].reshape(B, T, D)
```
